# Optimizing a Trainium2 kernel written in Bass

```python
import numpy as np
import jax
import jax.numpy as jnp

def _softmax(x, axis=-1):
    return jax.nn.softmax(x, axis=axis)

def _gelu(x):
    return jax.nn.gelu(x, approximate=True)

def _silu(x):
    return jax.nn.silu(x)

def _sigmoid(x):
    return jax.nn.sigmoid(x)

def _layernorm(x, axis=-1, eps=1e-05):
    m = jnp.mean(x, axis=axis, keepdims=True)
    v = jnp.var(x, axis=axis, keepdims=True)
    return (x - m) / jnp.sqrt(v + eps)

def _scatter_add(tgt, idx, src, axis=0):
    return tgt.at[idx].add(src)

def _segment_sum(src, seg, n):
    return jax.ops.segment_sum(src, seg, n)
kernel_name = 'mk_adaln_d1_jaxref_r8_7e6d00'

def setup_inputs(seed: int=0):
    np.random.seed(seed)
    _w = jnp.asarray

    def _L0_attn_setup():
        import jax, jax.numpy as jnp
        import numpy as np
        B, S, D = (8, 256, 128)
        EPS = 1e-07

        def _loc_weights(steps):
            idx = jnp.arange(steps)
            location = jnp.abs(idx[None, :] - idx[:, None]).astype(jnp.float32)
            lw = 1.0 / (location + EPS) * (location != 0).astype(jnp.float32)
            return lw
        key = jax.random.key(seed)
        kx, kw = jax.random.split(key)
        x = jax.random.normal(kx, (B, S, D), dtype=jnp.float32)
        limit = float(np.sqrt(6.0 / (D + D)))
        W = jax.random.uniform(kw, (D, D), dtype=jnp.float32, minval=-limit, maxval=limit)
        b = jnp.zeros((D,), dtype=jnp.float32)
        return {'x': x, 'W': W, 'b': b}
    _L0_attn_in = _L0_attn_setup()

    def _L0_ffn_setup():
        import jax, jax.numpy as jnp
        import numpy as np
        D_MODEL, D_FF, N_EXPERTS, TOP_K = (128, 512, 8, 2)
        BATCH, SEQ = (2, 256)
        key = jax.random.key(seed)
        ks = jax.random.split(key, 10)
        s = 0.02
        return {'x': jax.random.normal(ks[0], (BATCH, SEQ, D_MODEL), jnp.float32), 'Wg': jax.random.normal(ks[1], (D_MODEL, N_EXPERTS), jnp.float32) * s, 'W1': jax.random.normal(ks[2], (N_EXPERTS, D_MODEL, D_FF), jnp.float32) * s, 'b1': jnp.zeros((N_EXPERTS, D_FF), jnp.float32), 'W2': jax.random.normal(ks[3], (N_EXPERTS, D_FF, D_MODEL), jnp.float32) * s, 'b2': jnp.zeros((N_EXPERTS, D_MODEL), jnp.float32), 'Ws1': jax.random.normal(ks[4], (D_MODEL, D_FF), jnp.float32) * s, 'bs1': jnp.zeros((D_FF,), jnp.float32), 'Ws2': jax.random.normal(ks[5], (D_FF, D_MODEL), jnp.float32) * s, 'bs2': jnp.zeros((D_MODEL,), jnp.float32)}
    _L0_ffn_in = _L0_ffn_setup()
    _L0_c = _w((lambda *s: np.random.randn(*s).astype(np.float32) * 0.05)(8, 128))
    _L0_wmod = _w((lambda *s: np.random.randn(*s).astype(np.float32) * 0.05)(128, 6 * 128) * 128 ** (-0.5))
    _d = {'L0_attn_x': _L0_attn_in['x'], 'L0_attn_W': _L0_attn_in['W'], 'L0_attn_b': _L0_attn_in['b'], 'L0_ffn_Wg': _L0_ffn_in['Wg'], 'L0_ffn_W1': _L0_ffn_in['W1'], 'L0_ffn_b1': _L0_ffn_in['b1'], 'L0_ffn_W2': _L0_ffn_in['W2'], 'L0_ffn_b2': _L0_ffn_in['b2'], 'L0_ffn_Ws1': _L0_ffn_in['Ws1'], 'L0_ffn_bs1': _L0_ffn_in['bs1'], 'L0_ffn_Ws2': _L0_ffn_in['Ws2'], 'L0_ffn_bs2': _L0_ffn_in['bs2'], 'L0_c': _L0_c, 'L0_wmod': _L0_wmod}
    _x0 = _d['L0_attn_x']
    _d['L0_attn_x'] = jax.random.normal(jax.random.fold_in(jax.random.key(seed), 1), (8, 1024, 128), dtype=_x0.dtype)
    del _x0
    return _d

def reference(L0_attn_x, L0_attn_W, L0_attn_b, L0_ffn_Wg, L0_ffn_W1, L0_ffn_b1, L0_ffn_W2, L0_ffn_b2, L0_ffn_Ws1, L0_ffn_bs1, L0_ffn_Ws2, L0_ffn_bs2, L0_c, L0_wmod):

    def _L0_attn_ref(x, W, b):
        import jax, jax.numpy as jnp
        import numpy as np
        B, S, D = (8, 256, 128)
        EPS = 1e-07

        def _loc_weights(steps):
            idx = jnp.arange(steps)
            location = jnp.abs(idx[None, :] - idx[:, None]).astype(jnp.float32)
            lw = 1.0 / (location + EPS) * (location != 0).astype(jnp.float32)
            return lw
        steps = x.shape[1]
        x_tran = jnp.matmul(x, W) + b
        weights = jnp.einsum('bsd,btd->bst', x_tran, x)
        lw = _loc_weights(steps)
        weights = jnp.exp(jnp.tanh(weights * lw))
        off_diag = 1.0 - jnp.eye(steps, dtype=weights.dtype)
        weights = weights * off_diag
        weights = weights / (jnp.sum(weights, axis=-1, keepdims=True) + EPS)
        return jnp.matmul(weights, x)

    def _L0_ffn_ref(x, Wg, W1, b1, W2, b2, Ws1, bs1, Ws2, bs2):
        import jax, jax.numpy as jnp
        import numpy as np
        D_MODEL, D_FF, N_EXPERTS, TOP_K = (128, 512, 8, 2)
        BATCH, SEQ = (2, 256)
        B, S, D = x.shape
        xf = x.reshape(B * S, D)
        T = B * S
        logits = xf @ Wg
        top_vals, top_idx = jax.lax.top_k(logits, TOP_K)
        top_w = jax.nn.softmax(top_vals, axis=-1)
        combine = jnp.zeros((T, N_EXPERTS), x.dtype).at[jnp.arange(T)[:, None], top_idx].add(top_w)
        h = jax.nn.relu(jnp.einsum('td,edf->tef', xf, W1) + b1)
        sparse = jnp.einsum('te,tef,efd->td', combine, h, W2)
        sparse = sparse + combine @ b2
        shared = jax.nn.relu(xf @ Ws1 + bs1) @ Ws2 + bs2
        out = sparse + shared
        return out.reshape(B, S, D)
    x = L0_attn_x
    mod = (_silu(L0_c) @ L0_wmod).reshape(L0_c.shape[0], 6, 1, -1)
    sa, ca, ga, sb, cb, gb = (mod[:, 0], mod[:, 1], mod[:, 2], mod[:, 3], mod[:, 4], mod[:, 5])
    ga = (2 * (ga >= 0) - 1) * jnp.maximum(jnp.abs(ga), 0.25)
    gb = (2 * (gb >= 0) - 1) * jnp.maximum(jnp.abs(gb), 0.25)
    h = _layernorm(x, axis=-1) * (1 + ca) + sa
    x = x + ga * _L0_attn_ref(h, L0_attn_W, L0_attn_b)
    h = _layernorm(x, axis=-1) * (1 + cb) + sb
    x = x + gb * _L0_ffn_ref(h, L0_ffn_Wg, L0_ffn_W1, L0_ffn_b1, L0_ffn_W2, L0_ffn_b2, L0_ffn_Ws1, L0_ffn_bs1, L0_ffn_Ws2, L0_ffn_bs2)
    return x

_drawn_inputs = setup_inputs


def setup_inputs(seed=0):
    import zlib

    import numpy as np

    out = dict(_drawn_inputs(seed))
    spreads = {'L0_attn_b': (0.0, 0.8),
     'L0_ffn_b1': (0.0, 0.8),
     'L0_ffn_b2': (0.0, 0.462),
     'L0_ffn_bs1': (0.0, 0.8),
     'L0_ffn_bs2': (0.0, 0.336)}
    factors = {'L0_attn_W': 8.0,
     'L0_ffn_Wg': 2.872,
     'L0_ffn_W1': 5.207,
     'L0_ffn_W2': 4.073,
     'L0_ffn_Ws1': 3.706,
     'L0_ffn_Ws2': 2.849}
    for name, (base, spread) in spreads.items():
        noise = np.random.default_rng([zlib.crc32(name.encode()), seed]).standard_normal(out[name].shape)
        drawn = base * np.exp(spread * noise) if base else spread * noise
        out[name] = jnp.asarray(drawn.astype(out[name].dtype))
    for name, factor in factors.items():
        out[name] = (out[name] * factor).astype(out[name].dtype)
    return out
```

```python
from contextlib import ExitStack

import numpy as np

import concourse.bass as bass
from concourse import mybir

F32 = mybir.dt.float32
I32 = mybir.dt.int32
U32 = mybir.dt.uint32
ALU = mybir.AluOpType
ACT = mybir.ActivationFunctionType
AX = mybir.AxisListType

P = 128
B, S, D = 8, 1024, 128
G = S // P
T = B * S
E, F = 8, 512
C = F // P
TILE = 512
K = TILE // P
REGION = T + TILE
ROW = D + 2
ROW_TILES = 2 * T // TILE + E - 1
SPARE = E * REGION
X_ROWS = SPARE + TILE
Z_ROWS = 2 * T
NOWHERE = 2 * Z_ROWS
W2_AT, B1_AT, B2_AT = F, F + C * D, F + C * D + C
PACK = B2_AT + D
MOD = 6 * D
EPS_ATT = 1e-7
EPS_LN = 1e-5
SHARED_TILES = T // TILE
RING = 3
assert ROW_TILES % RING == 0


class Chain:

    def __init__(self, eng, sem, start):
        self.eng, self.sem, self.start, self.n = eng, sem, start, 0

    def __call__(self, ins, wait=True):
        ins.then_inc(self.sem, 1)
        self.n += 1
        if wait:
            self.eng.wait_ge(self.sem, self.now())

    def now(self):
        return self.start + self.n


def adaln_moe(nc, x, c_t, wmod, w_att, b_att, wg, packs, out):
    with ExitStack() as ctx:
        def sb(name, shape, dt=F32):
            return ctx.enter_context(nc.sbuf_tensor(name, shape, dt))

        def ps(name, shape):
            return ctx.enter_context(nc.psum_tensor(name, shape, F32))

        def sem(name):
            return ctx.enter_context(nc.semaphore(name))

        rows_x = nc.dram_tensor("rows_x", [X_ROWS, ROW], F32).ap()
        rows_z = nc.dram_tensor("rows_z", [Z_ROWS, D], F32).ap()

        ident = sb("ident", [P, P])
        offdiag = sb("offdiag", [P, P])
        before = sb("before", [P, P])
        ones = sb("ones", [P, P])
        lw = sb("lw", [P, (2 * G - 1) * P])
        minus_half = sb("minus_half", [P, G])
        expert_no = sb("expert_no", [P, G, E])
        token_no = sb("token_no", [P, G])
        region_at = sb("region_at", [P, E])
        tile_no = sb("tile_no", [P, ROW_TILES, E])
        pad_rows = sb("pad_rows", [P, K, ROW])
        c_sb = sb("c_sb", [P, B])
        silu = sb("silu", [P, B])
        wmod_sb = sb("wmod_sb", [P, MOD])
        watt_sb = sb("watt_sb", [D, D])
        batt_sb = sb("batt_sb", [D, 1])
        wg_sb = sb("wg_sb", [D, E])
        w_shared = sb("w_shared", [P, PACK])
        w_exp = [sb(f"w_exp{i}", [P, PACK]) for i in range(RING)]
        mod = sb("mod", [P, B, 6, D])
        res = sb("res", [P, B * G, D])
        h2_t = sb("h2_t", [D, T])
        lw_mask = h2_t[:, 0:(2 * G - 1) * P]
        stats = sb("stats", [P, G, 6])
        moments = sb("moments", [P, G, 2])
        rstd = sb("rstd", [P, G])
        stats2 = sb("stats2", [P, G, 6])
        moments2 = sb("moments2", [P, G, 2])
        rstd2 = sb("rstd2", [P, G])
        xhat = sb("xhat", [P, G, D])
        xhat2 = sb("xhat2", [P, G, D])
        res_tmp = sb("res_tmp", [P, G, D])
        silu_b = res_tmp
        h_sb = sb("h_sb", [P, G, D])
        h_ones = sb("h_ones", [P, 2, G, D + 1])
        work = sb("work", [P, RING * C * TILE])
        prob = work[:, 0:4 * S].rearrange("p (t s) -> p t s", t=4)
        h_t = work[:, 4 * S:5 * S]
        q_t = work[:, 5 * S:6 * S]
        den = sb("den", [P, G])
        rden = sb("rden", [P, G])
        row_1 = sb("row_1", [P, G, ROW])
        row_2 = sb("row_2", [P, G, ROW])
        h2_ts = sb("h2_ts", [D, S])
        logits = sb("logits", [P, G, E])
        top_v = sb("top_v", [P, G, E])
        top_i = sb("top_i", [P, G, E], U32)
        top_f = sb("top_f", [P, G, E])
        hot_1 = sb("hot_1", [P, G, E])
        hot_2 = sb("hot_2", [P, G, E])
        chosen = sb("chosen", [P, G, E])
        earlier = sb("earlier", [P, G + 1, E])
        carry = sb("carry", [P, E])
        place = sb("place", [P, G, E])
        slot_f = sb("slot_f", [P, 2, G])
        slot = sb("slot", [P, 2, G], I32)
        gap = sb("gap", [P, G])
        gap_e = sb("gap_e", [P, G])
        gap_1 = sb("gap_1", [P, G])
        w_first = sb("w_first", [P, G])
        w_second = sb("w_second", [P, G])
        count = sb("count", [P, E])
        count_i = sb("count_i", [P, E], I32)
        tiles_i = sb("tiles_i", [P, E], I32)
        tiles_f = sb("tiles_f", [P, E])
        ends = sb("ends", [P, E])
        starts = sb("starts", [P, E])
        past = sb("past", [P, ROW_TILES, E])
        tile_e = sb("tile_e", [P, ROW_TILES])
        tile_s = sb("tile_s", [P, ROW_TILES])
        tile_u = sb("tile_u", [P, ROW_TILES])
        tile_r = sb("tile_r", [P, ROW_TILES])
        table_e = sb("table_e", [P, ROW_TILES], I32)
        table_r = sb("table_r", [P, ROW_TILES], I32)
        pad_at = sb("pad_at", [P, E], I32)
        tile_x = [sb(f"tile_x{i}", [P, K, ROW]) for i in range(RING)]
        tile_xt = sb("tile_xt", [D, TILE])
        hidden = [work[:, i * C * TILE:(i + 1) * C * TILE].rearrange("p (c n) -> p c n", c=C) for i in range(RING)]
        tile_y = [sb(f"tile_y{i}", [P, K, D]) for i in range(RING)]

        score = ps("score", [P, 4, 512])
        value = ps("value", [P, 3, 512])
        misc = ps("misc", [P, 512])
        yacc = [value[:, 0, :], value[:, 1, :], misc[:, :]]
        xt_ps = value[:, 2, :]

        def value_at(s):
            return value[:, s // 3, (s % 3) * (D + 1):(s % 3) * (D + 1) + D]

        loaded = sem("loaded")
        const_ready = sem("const_ready")
        const_step = sem("const_step")
        places_passed = sem("places_passed")
        silu_step = sem("silu_step")
        silu_exp = sem("silu_exp")
        silu_ready = sem("silu_ready")
        mod_ps_ready = sem("mod_ps_ready")
        mod_evac = sem("mod_evac")
        mod_step = sem("mod_step")
        mod_ready = sem("mod_ready")

        ln1_step = sem("ln1_step")
        ln1_moments = sem("ln1_moments")
        ln1_pool_step = sem("ln1_pool_step")
        ln1_mod_step = sem("ln1_mod_step")
        ln2_mod_step = sem("ln2_mod_step")
        ln1_rstd = sem("ln1_rstd")
        ln1_xhat = sem("ln1_xhat")
        ln1_h = sem("ln1_h")
        values_ready = sem("values_ready")
        ht_ps_ready = sem("ht_ps_ready")
        ht_ready = sem("ht_ready")
        qt_ps_ready = sem("qt_ps_ready")
        qt_ready = sem("qt_ready")
        score_ready = sem("score_ready")
        score_used = sem("score_used")
        tanh_done = sem("tanh_done")
        exp_done = sem("exp_done")
        prob_ready = sem("prob_ready")
        value_step = sem("value_step")
        value_used = sem("value_used")
        att_step = sem("att_step")
        ln2_step = sem("ln2_step")
        ln2_moments = sem("ln2_moments")
        ln2_pool_step = sem("ln2_pool_step")
        ln2_rstd = sem("ln2_rstd")
        ln2_xhat = sem("ln2_xhat")
        ln2_h = sem("ln2_h")
        second_rows = sem("second_rows")
        h2t_ps_ready = sem("h2t_ps_ready")
        h2t_staged = sem("h2t_staged")
        h2t_kept = sem("h2t_kept")
        logits_ps_ready = sem("logits_ps_ready")
        logits_ready = sem("logits_ready")
        route_step = sem("route_step")
        chosen_ready = sem("chosen_ready")
        gap_ready = sem("gap_ready")
        gap_exp = sem("gap_exp")
        rank_ps_ready = sem("rank_ps_ready")
        rank_used = sem("rank_used")
        slots_ready = sem("slots_ready")
        scattered = sem("scattered")

        total_ps_ready = sem("total_ps_ready")
        table_step = sem("table_step")
        table_ready = sem("table_ready")
        padded = sem("padded")
        x_loaded = [sem(f"x_loaded{i}") for i in range(RING)]
        w_loaded = [sem(f"w_loaded{i}") for i in range(RING)]
        xt_ps_ready = sem("xt_ps_ready")
        xt_ready = sem("xt_ready")
        up_ready = sem("up_ready")
        hidden_ready = sem("hidden_ready")
        down_ready = sem("down_ready")
        y_evac = sem("y_evac")
        y_step = sem("y_step")
        y_ready = sem("y_ready")
        y_sent = [sem(f"y_sent{i}") for i in range(RING)]
        z_loaded = [sem(f"z_loaded{i}") for i in range(2)]
        fin_step = sem("fin_step")
        fin_ready = sem("fin_ready")
        stored = sem("stored")

        x_v = x.rearrange("(b p g) d -> p b (g d)", b=B, p=P, g=G)
        out_v = out.rearrange("(b p g) d -> b p (g d)", b=B, p=P, g=G)
        z_v = rows_z.rearrange("(k b p g) d -> k b p (g d)", k=2, b=B, p=P, g=G)
        N_LOADS = 6 + B
        ROUTE, ATT = 26, 3

        z_buf = [[hidden[i][:, 2 * k:2 * k + 2, :].rearrange("p c n -> p (c n)") for k in range(2)] for i in range(2)]

        block = ctx.enter_context(nc.Block())

        def wait_alone(eng, *waits):
            for on, v in waits:
                eng.wait_ge(on, v)
                eng.sem_inc(places_passed, 1)

        @block.sync
        def _(sp):
            for b in range(B):
                sp.dma_start(res[:, b * G:(b + 1) * G, :].rearrange("p g d -> p (g d)"), x_v[:, b, :]).then_inc(loaded, 16)
            sp.dma_start(w_shared[:, :], packs[E]).then_inc(loaded, 16)

            sp.wait_ge(table_ready, 1)
            sp.wait_ge(scattered, 16 * 2 * G * B)
            sp.wait_ge(const_ready, 1)
            for e in range(E):
                at = sp.value_load(pad_at[0:1, e:e + 1], min_val=0, max_val=SPARE - TILE)
                sp.dma_start(rows_x[bass.ds(at, TILE), :].rearrange("(p k) r -> p (k r)", p=P),
                             pad_rows[:, :, :].rearrange("p k r -> p (k r)")).then_inc(padded, 16)
            sp.dma_start(rows_x[SPARE:X_ROWS, :].rearrange("(p k) r -> p (k r)", p=P),
                         pad_rows[:, :, :].rearrange("p k r -> p (k r)")).then_inc(padded, 16)
            sp.wait_ge(padded, 16 * (E + 1))

            def load_tile(j, i, par, first):
                if not first:
                    wait_alone(sp, (y_sent[par], 16 * K * i), (y_evac, SHARED_TILES + j - RING + 1))
                e = sp.value_load(table_e[0:1, bass.ds(j, 1)], min_val=0, max_val=E - 1)
                r = sp.value_load(table_r[0:1, bass.ds(j, 1)], min_val=0, max_val=SPARE)
                sp.dma_start(tile_x[par][:, :, :].rearrange("p k r -> p (k r)"),
                             rows_x[bass.ds(r, TILE), :].rearrange("(p k) r -> p (k r)", p=P)).then_inc(x_loaded[par], 16)
                sp.dma_start(w_exp[par][:, :], packs[bass.ds(e, 1), :, :].rearrange("e p n -> (e p) n")).then_inc(w_loaded[par], 16)

            for par in range(RING):
                load_tile(par, 0, par, True)
            with sp.Fori(1, ROW_TILES // RING) as i:
                for par in range(RING):
                    load_tile(RING * i + par, i, par, False)

            for par in range(RING):
                sp.wait_ge(y_sent[par], 16 * K * (ROW_TILES // RING))

            def load_results(b, par):
                for k in range(2):
                    sp.dma_start(z_buf[par][k], z_v[k, bass.ds(b, 1), :, :].rearrange("b p n -> (b p) n")).then_inc(z_loaded[par], 16)

            def store(b):
                sp.wait_ge(fin_ready, b + 1)
                sp.dma_start(out_v[bass.ds(b, 1), :, :].rearrange("b p n -> (b p) n"),
                             res[:, bass.ds(b * G, G), :].rearrange("p g d -> p (g d)")).then_inc(stored, 16)

            for b in range(2):
                load_results(b, b)
            with sp.Fori(0, B // 2 - 1) as i:
                for par in range(2):
                    store(2 * i + par)
                    load_results(2 * i + par + 2, par)
            for b in range(B - 2, B):
                store(b)
            sp.wait_ge(stored, 16 * B)

        @block.gpsimd
        def _(pool):
            step = Chain(pool, const_step, 0)
            step(nc.gpsimd.memset(ident[:, :], 0.0), wait=False)
            step(nc.gpsimd.memset(offdiag[:, :], 1.0), wait=False)
            step(nc.gpsimd.memset(before[:, :], 1.0), wait=False)
            step(nc.gpsimd.memset(pad_rows[:, :, :], 0.0), wait=False)
            step(nc.gpsimd.iota(lw_mask[:, :].rearrange("p (g q) -> p g q", q=P), pattern=[[1, 2 * G - 1], [G, P]],
                                base=-(G - 1), channel_multiplier=-G, allow_small_or_imprecise_dtypes=True))
            step(nc.gpsimd.affine_select(out=ident[:, :], in_=ident[:, :], compare_op=ALU.not_equal, fill=1.0,
                                         base=0, pattern=[[-1, P]], channel_multiplier=1), wait=False)
            step(nc.gpsimd.affine_select(out=offdiag[:, :], in_=offdiag[:, :], compare_op=ALU.not_equal, fill=0.0,
                                         base=0, pattern=[[-1, P]], channel_multiplier=1), wait=False)
            step(nc.gpsimd.affine_select(out=before[:, :], in_=before[:, :], compare_op=ALU.is_gt, fill=0.0,
                                         base=0, pattern=[[1, P]], channel_multiplier=-1), wait=False)
            step(nc.gpsimd.memset(ones[:, :], 1.0), wait=False)
            step(nc.gpsimd.memset(minus_half[:, :], -0.5), wait=False)
            step(nc.gpsimd.memset(h_ones[:, :, :, D:D + 1], 1.0), wait=False)
            step(nc.gpsimd.memset(carry[:, :], 0.0), wait=False)
            step(nc.gpsimd.memset(earlier[:, 0, :], 0.0), wait=False)
            step(nc.gpsimd.iota(expert_no[:, :, :], pattern=[[0, G], [1, E]], base=0, channel_multiplier=0,
                                allow_small_or_imprecise_dtypes=True), wait=False)
            step(nc.gpsimd.iota(token_no[:, :], pattern=[[1, G]], base=0, channel_multiplier=G,
                                allow_small_or_imprecise_dtypes=True), wait=False)
            step(nc.gpsimd.iota(region_at[:, :], pattern=[[REGION, E]], base=0, channel_multiplier=0,
                                allow_small_or_imprecise_dtypes=True), wait=False)
            step(nc.gpsimd.iota(tile_no[:, :, :], pattern=[[1, ROW_TILES], [0, E]], base=0, channel_multiplier=0,
                                allow_small_or_imprecise_dtypes=True), wait=False)
            step(nc.gpsimd.iota(pad_rows[:, :, D:D + 1].bitcast(I32), pattern=[[0, K]], base=NOWHERE, channel_multiplier=0))
            nc.gpsimd.tensor_copy(carry[0:1, :], region_at[0:1, :]).then_inc(const_ready, 1)

            def rstd_of(mom, rs, ready, chain, done, b):
                wait_alone(pool, (ready, b + 1))
                step = Chain(pool, chain, b)
                step(nc.gpsimd.tensor_scalar(rs[:, :], mom[:, :, 1], EPS_LN, None, ALU.add))
                nc.gpsimd.tensor_tensor(rs[:, :], rs[:, :], minus_half[:, :], ALU.pow).then_inc(done, 1)

            def modulate(xh, dst, ready, chain, done, b, at):
                pool.wait_ge(ready, b + 1)
                step = Chain(pool, chain, b)
                scale = mod[:, bass.ds(b, 1), at + 1, :].to_broadcast([P, G, D])
                shift = mod[:, bass.ds(b, 1), at, :].to_broadcast([P, G, D])
                step(nc.gpsimd.tensor_tensor(xh[:, :, :], xh[:, :, :], scale, ALU.mult))
                nc.gpsimd.tensor_tensor(dst, xh[:, :, :], shift, ALU.add).then_inc(done, 1)

            def norm_1(b, first):
                rstd_of(moments, rstd, ln1_moments, ln1_pool_step, ln1_rstd, b)

            def mod_1(b, first):
                if not first:
                    pool.wait_ge(ht_ps_ready, 2 * b)
                    pool.wait_ge(values_ready, b)
                modulate(xhat, h_sb[:, :, :], ln1_xhat, ln1_mod_step, ln1_h, b, 0)

            def mod_2(b, first):
                if not first:
                    pool.wait_ge(scattered, 16 * 2 * G * b)
                    pool.wait_ge(h2t_ps_ready, 2 * b)
                    pool.wait_ge(second_rows, b)
                modulate(xhat2, row_1[:, :, 0:D], ln2_xhat, ln2_mod_step, ln2_h, b, 3)

            def scatter(b):
                wait_alone(pool, (slots_ready, b + 1), (second_rows, b + 1))
                for k, rows in enumerate((row_1, row_2)):
                    for g in range(G):
                        nc.gpsimd.indirect_dma_start(rows_x[:, :], bass.IndirectOffsetOnAxis(ap=slot[:, k, g:g + 1], axis=0),
                                                     rows[:, g, :], None).then_inc(scattered, 16)

            pool.wait_ge(mod_ready, 1)
            norm_1(0, True)
            mod_1(0, True)
            norm_1(1, False)
            mod_1(1, False)

            def batch(b, first=False, last=False):
                rstd_of(moments2, rstd2, ln2_moments, ln2_pool_step, ln2_rstd, b - 1)
                mod_2(b - 1, first)
                if not last:
                    norm_1(b + 1, False)
                    mod_1(b + 1, False)
                scatter(b - 1)

            batch(1, first=True)
            with pool.Fori(2, B - 1) as b:
                batch(b)
            batch(B - 1, last=True)
            rstd_of(moments2, rstd2, ln2_moments, ln2_pool_step, ln2_rstd, B - 1)
            mod_2(B - 1, False)
            scatter(B - 1)

            def send(j, par):
                wait_alone(pool, (y_ready, j + 1))
                for k in range(K):
                    nc.gpsimd.indirect_dma_start(rows_z[:, :], bass.IndirectOffsetOnAxis(ap=tile_x[par][:, k, D:D + 1].bitcast(I32), axis=0),
                                                 tile_y[par][:, k, :], None, bounds_check=Z_ROWS - 1, oob_is_err=False).then_inc(y_sent[par], 16)

            with pool.Fori(0, ROW_TILES // RING) as i:
                for par in range(RING):
                    send(RING * i + par, par)

        @block.scalar
        def _(act):
            act.dma_start(c_sb[:, :], c_t).then_inc(loaded, 16)
            act.dma_start(wmod_sb[:, :], wmod).then_inc(loaded, 16)
            act.dma_start(watt_sb[:, :], w_att).then_inc(loaded, 16)
            act.dma_start(batt_sb[:, :], b_att).then_inc(loaded, 16)
            act.dma_start(wg_sb[:, :], wg).then_inc(loaded, 16)
            act.wait_ge(loaded, 16 * N_LOADS)
            nc.scalar.activation(silu[:, :], c_sb[:, :], ACT.Exp, scale=-1.0).then_inc(silu_exp, 1)
            for n in range(2 * B):
                act.wait_ge(mod_ps_ready, n + 1)
                nc.scalar.activation(mod[:, n // 2, 3 * (n % 2):3 * (n % 2) + 3, :].rearrange("p m d -> p (m d)"),
                                     score[:, n % 4, 0:MOD // 2], ACT.Copy).then_inc(mod_evac, 1)

            def copy_values(b, first):
                act.wait_ge(ln1_h, b + 1)
                if not first:
                    act.wait_ge(value_step, G * (b - 1))
                nc.scalar.activation(h_ones[:, bass.ds(b % 2, 1), :, 0:D].rearrange("p o g d -> p (o g) d"), h_sb[:, :, :],
                                     ACT.Copy).then_inc(values_ready, 1)

            def transposed(b, first):
                if not first:
                    act.wait_ge(score_ready, G * b)
                for half in range(2):
                    act.wait_ge(ht_ps_ready, 2 * b + half + 1)
                    nc.scalar.activation(h_t[:, half * 512:half * 512 + 512], misc[:, :], ACT.Copy).then_inc(ht_ready, 1)

            def queries(b):
                for half in range(2):
                    act.wait_ge(qt_ps_ready, 2 * b + half + 1)
                    nc.scalar.activation(q_t[:, half * 512:half * 512 + 512], misc[:, :], ACT.Identity,
                                         bias=batt_sb[:, 0:1]).then_inc(qt_ready, 1)

            def weights(b, t):
                act.wait_ge(score_used, G * b + t + 1)
                nc.scalar.activation(prob[:, t % 4, :], prob[:, t % 4, :], ACT.Tanh).then_inc(tanh_done, 1)
                act.wait_ge(tanh_done, G * b + t + 1)
                nc.scalar.activation(prob[:, t % 4, :], prob[:, t % 4, :], ACT.Exp).then_inc(exp_done, 1)

            def second_copy(b, first):
                act.wait_ge(ln2_h, b + 1)
                if not first:
                    act.wait_ge(scattered, 16 * 2 * G * b)
                nc.scalar.activation(row_2[:, :, 0:D], row_1[:, :, 0:D], ACT.Copy).then_inc(second_rows, 1)

            def stage_h2t(b, half, first):
                act.wait_ge(h2t_ps_ready, 2 * b + half + 1)
                if not first:
                    act.wait_ge(logits_ps_ready, b)
                nc.scalar.activation(h2_ts[:, half * 512:half * 512 + 512], misc[:, :], ACT.Copy).then_inc(h2t_staged, 1)

            def keep_h2t(b):
                act.wait_ge(h2t_staged, 2 * b + 2)
                nc.scalar.activation(h2_t[:, bass.ds(b * S, S)], h2_ts[:, :], ACT.Copy).then_inc(h2t_kept, 1)

            def gap_exponent(b):
                act.wait_ge(gap_ready, b + 1)
                nc.scalar.activation(gap_e[:, :], gap[:, :], ACT.Exp).then_inc(gap_exp, 1)

            def batch(b, first=False, second=False, last=False):
                for t in range(G):
                    weights(b, t)
                    if t == 3 and not first:
                        second_copy(b - 1, second)
                    if t == 4 and not first:
                        stage_h2t(b - 1, 0, second)
                        stage_h2t(b - 1, 1, second)
                        keep_h2t(b - 1)
                    if t == 4 and not last:
                        copy_values(b + 1, first)
                    if t == 6 and not first:
                        gap_exponent(b - 1)
                if not last:
                    transposed(b + 1, False)
                    queries(b + 1)

            copy_values(0, True)
            transposed(0, True)
            queries(0)
            batch(0, first=True)
            batch(1, second=True)
            with act.Fori(2, B - 1) as b:
                batch(b)
            batch(B - 1, last=True)
            second_copy(B - 1, False)
            stage_h2t(B - 1, 0, False)
            stage_h2t(B - 1, 1, False)
            keep_h2t(B - 1)
            gap_exponent(B - 1)

            def relu(n, w, par):
                for c in range(C):
                    act.wait_ge(up_ready, C * n + c + 1)
                    nc.scalar.activation(hidden[par][:, c, :], score[:, c, :], ACT.Relu,
                                         bias=w[:, B1_AT + c:B1_AT + c + 1]).then_inc(hidden_ready, 1)

            with act.Fori(0, SHARED_TILES // 2) as i:
                for par in range(2):
                    relu(2 * i + par, w_shared, par)

            def expert(j, par):
                act.wait_ge(xt_ps_ready, j + 1)
                act.wait_ge(up_ready, C * (SHARED_TILES + j))
                nc.scalar.activation(tile_xt[:, :], xt_ps, ACT.Copy).then_inc(xt_ready, 1)
                relu(SHARED_TILES + j, w_exp[par], par)

            with act.Fori(0, ROW_TILES // RING) as i:
                for par in range(RING):
                    expert(RING * i + par, par)

        @block.vector
        def _(dve):
            step = Chain(dve, silu_step, 0)
            dve.wait_ge(silu_exp, 1)
            step(nc.vector.tensor_scalar(silu[:, :], silu[:, :], 1.0, None, ALU.add))
            step(nc.vector.reciprocal(silu[:, :], silu[:, :]))
            step(nc.vector.tensor_tensor(silu[:, :], silu[:, :], c_sb[:, :], ALU.mult))
            nc.vector.tensor_copy(silu_b[:, :, :], silu[:, :].rearrange("p (b o) -> p b o", o=1).to_broadcast([P, B, P])).then_inc(silu_ready, 1)
            dve.wait_ge(const_ready, 1)
            step(nc.vector.scalar_tensor_tensor(out=lw[:, :], in0=lw_mask[:, :], scalar=-1.0, in1=lw_mask[:, :], op0=ALU.mult, op1=ALU.max))
            step(nc.vector.tensor_scalar(lw_mask[:, :], lw[:, :], 0.0, None, ALU.is_gt))
            step(nc.vector.tensor_scalar(lw[:, :], lw[:, :], EPS_ATT, None, ALU.add))
            step(nc.vector.reciprocal(lw[:, :], lw[:, :]))
            step(nc.vector.tensor_tensor(lw[:, :], lw[:, :], lw_mask[:, :], ALU.mult))
            dve.wait_ge(mod_evac, 2 * B)
            step = Chain(dve, mod_step, 0)
            for at in (0, 3):
                scale, gate = mod[:, :, at + 1, :], mod[:, :, at + 2, :]
                sign = res_tmp[:, :, :]
                step(nc.vector.tensor_scalar(scale, scale, 1.0, None, ALU.add))
                step(nc.vector.tensor_scalar(sign, gate, 0.0, 2.0, ALU.is_ge, ALU.mult))
                step(nc.vector.scalar_tensor_tensor(out=gate, in0=gate, scalar=-1.0, in1=gate, op0=ALU.mult, op1=ALU.max))
                step(nc.vector.tensor_scalar(sign, sign, -1.0, None, ALU.add))
                step(nc.vector.scalar_tensor_tensor(out=gate, in0=gate, scalar=0.25, in1=sign, op0=ALU.max, op1=ALU.mult))
            dve.wait_ge(loaded, 16 * N_LOADS)
            nc.vector.memset(den[:, :], 0.0).then_inc(mod_ready, 1)

            def moments_of(b, st, mom, chain, done, rows):
                step = Chain(dve, chain, b)
                wait_alone(dve, rows)
                for g in range(G):
                    ins = nc.vector.bn_stats(st[:, g, :], res[:, bass.ds(b * G + g, 1), :].rearrange("p o d -> p (o d)"))
                step(ins, wait=False)
                wait_alone(dve, (step.sem, step.now()))
                for g in range(G):
                    ins = nc.vector.bn_aggr(mom[:, g, :], st[:, g, :])
                ins.then_inc(done, 1)

            def normalise(b, mom, rs, xh, ready, done, used, first=False):
                dve.wait_ge(ready, b + 1)
                if not first:
                    dve.wait_ge(used, b)
                for g in range(G):
                    ins = nc.vector.tensor_scalar(xh[:, g, :], res[:, bass.ds(b * G + g, 1), :].rearrange("p o d -> p (o d)"),
                                                  mom[:, g, 0:1], rs[:, g:g + 1], ALU.subtract, ALU.mult)
                ins.then_inc(done, 1)

            def weigh(b, t, first):
                dve.wait_ge(score_ready, G * b + t + 1)
                if not (first and t < 4):
                    dve.wait_ge(value_step, G * b + t - 3)
                at = (G - 1 - t) * P
                nc.vector.tensor_tensor(prob[:, t % 4, :].rearrange("p (h n) -> p h n", h=2), score[:, 2 * (t % 2):2 * (t % 2) + 2, :],
                                        lw[:, at:at + S].rearrange("p (h n) -> p h n", h=2), ALU.mult).then_inc(score_used, 1)

            def clear_diagonal(b, t):
                dve.wait_ge(exp_done, G * b + t + 1)
                own = prob[:, t % 4, t * P:(t + 1) * P]
                nc.vector.tensor_tensor(own, own, offdiag[:, :], ALU.mult).then_inc(prob_ready, 1)

            def attend(b):
                dve.wait_ge(value_step, G * b + G)
                step = Chain(dve, att_step, ATT * b)
                for i in range(3):
                    n = min(3, G - 3 * i)
                    col = value[:, i, 0:n * (D + 1)].rearrange("p (s d) -> p s d", d=D + 1)[:, :, D]
                    ins = nc.vector.tensor_scalar(den[:, 3 * i:3 * i + n], col, EPS_ATT, None, ALU.add)
                step(ins)
                step(nc.vector.reciprocal(rden[:, :], den[:, :]))
                gate = mod[:, bass.ds(b, 1), 2, :].rearrange("p o d -> p (o d)")
                for s in range(G):
                    ins = nc.vector.scalar_tensor_tensor(out=res_tmp[:, s, :], in0=value_at(s), scalar=rden[:, s:s + 1], in1=gate,
                                                         op0=ALU.mult, op1=ALU.mult)
                ins.then_inc(value_used, 1)
                dve.wait_ge(value_used, b + 1)
                r = res[:, bass.ds(b * G, G), :]
                step(nc.vector.tensor_tensor(r, r, res_tmp[:, :, :], ALU.add), wait=False)

            def choose(b, first):
                dve.wait_ge(logits_ps_ready, b + 1)
                step = Chain(dve, route_step, ROUTE * b)
                nc.vector.tensor_copy(logits[:, :, :].rearrange("p g e -> p (g e)"), misc[:, 0:G * E]).then_inc(logits_ready, 1)
                wait_alone(dve, (logits_ready, b + 1))
                for g in range(G):
                    ins = nc.vector.max(top_v[:, g, :], logits[:, g, :])
                step(ins, wait=False)
                wait_alone(dve, (step.sem, step.now()))
                for g in range(G):
                    ins = nc.vector.max_index(top_i[:, g, :], top_v[:, g, :], logits[:, g, :])
                step(ins, wait=False)
                nc.vector.tensor_tensor(gap[:, :], top_v[:, :, 1], top_v[:, :, 0], ALU.subtract).then_inc(gap_ready, 1)
                dve.wait_ge(route_step, ROUTE * b + step.n)
                step(nc.vector.tensor_copy(top_f[:, :, :], top_i[:, :, :]))
                step(nc.vector.tensor_tensor(hot_1[:, :, :], expert_no[:, :, :], top_f[:, :, 0:1].to_broadcast([P, G, E]), ALU.is_equal), wait=False)
                step(nc.vector.tensor_tensor(hot_2[:, :, :], expert_no[:, :, :], top_f[:, :, 1:2].to_broadcast([P, G, E]), ALU.is_equal))
                step(nc.vector.tensor_tensor(chosen[:, :, :], hot_1[:, :, :], hot_2[:, :, :], ALU.add))
                if not first:
                    dve.wait_ge(rank_ps_ready, b)
                for g in range(G):
                    ins = nc.vector.tensor_tensor(earlier[:, g + 1, :], earlier[:, g, :], chosen[:, g, :], ALU.add)
                    if g < G - 1:
                        step(ins)
                ins.then_inc(chosen_ready, 1)
                return step.n

            def assign(b, done):
                step = Chain(dve, route_step, ROUTE * b)
                step.n = done
                dve.wait_ge(rank_ps_ready, b + 1)
                rank = misc[:, 0:E].rearrange("p (o e) -> p o e", o=1).to_broadcast([P, G, E])
                nc.vector.tensor_tensor(place[:, :, :], earlier[:, 0:G, :], rank, ALU.add).then_inc(rank_used, 1)
                step(nc.vector.tensor_tensor(carry[:, :], carry[:, :], earlier[:, G, :], ALU.add), wait=False)
                dve.wait_ge(rank_used, b + 1)
                step(nc.vector.tensor_tensor(hot_1[:, :, :], hot_1[:, :, :], place[:, :, :], ALU.mult), wait=False)
                step(nc.vector.tensor_tensor(hot_2[:, :, :], hot_2[:, :, :], place[:, :, :], ALU.mult))
                step(nc.vector.tensor_reduce(slot_f[:, 0, :], hot_1[:, :, :], AX.X, ALU.add), wait=False)
                step(nc.vector.tensor_reduce(slot_f[:, 1, :], hot_2[:, :, :], AX.X, ALU.add))
                dve.wait_ge(gap_exp, b + 1)
                step(nc.vector.tensor_scalar(gap_1[:, :], gap_e[:, :], 1.0, None, ALU.add))
                step(nc.vector.reciprocal(w_first[:, :], gap_1[:, :]))
                step(nc.vector.tensor_tensor(w_second[:, :], w_first[:, :], gap_e[:, :], ALU.mult))
                dve.wait_ge(ln2_h, b + 1)
                step(nc.vector.tensor_copy(slot[:, :, :], slot_f[:, :, :]), wait=False)
                step(nc.vector.tensor_copy(row_1[:, :, D + 1], w_first[:, :]), wait=False)
                step(nc.vector.tensor_copy(row_2[:, :, D + 1], w_second[:, :]), wait=False)
                step(nc.vector.tensor_copy(row_1[:, :, D].bitcast(I32), token_no[:, :]), wait=False)
                step(nc.vector.tensor_scalar(row_2[:, :, D].bitcast(I32), token_no[:, :], float(T), None, ALU.add))
                nc.vector.tensor_scalar(token_no[:, :], token_no[:, :], float(S), None, ALU.add).then_inc(slots_ready, 1)
                dve.wait_ge(slots_ready, b + 1)
                assert step.n == ROUTE, step.n

            def batch(b, first=False, second=False, last=False):
                done = 0
                for t in range(G):
                    weigh(b, t, first)
                    if t > 0:
                        clear_diagonal(b, t - 1)
                    if t == 1 and not first:
                        attend(b - 1)
                        moments_of(b - 1, stats2, moments2, ln2_step, ln2_moments, (att_step, ATT * b))
                    if t == 2 and not first:
                        normalise(b - 1, moments2, rstd2, xhat2, ln2_rstd, ln2_xhat, ln2_h, second)
                    if t == 3 and not last:
                        if not first:
                            moments_of(b + 1, stats, moments, ln1_step, ln1_moments, (loaded, 16 * N_LOADS))
                    if t == 4 and not last:
                        if not first:
                            normalise(b + 1, moments, rstd, xhat, ln1_rstd, ln1_xhat, ln1_h)
                    if t == 5 and not first:
                        done = choose(b - 1, second)
                    if t == 7 and not first:
                        assign(b - 1, done)
                clear_diagonal(b, G - 1)

            def norm_first(b):
                moments_of(b, stats, moments, ln1_step, ln1_moments, (loaded, 16 * N_LOADS))
                normalise(b, moments, rstd, xhat, ln1_rstd, ln1_xhat, ln1_h, b == 0)

            norm_first(0)
            norm_first(1)
            batch(0, first=True)
            batch(1, second=True)
            with dve.Fori(2, B - 1) as b:
                batch(b)
            batch(B - 1, last=True)
            attend(B - 1)
            moments_of(B - 1, stats2, moments2, ln2_step, ln2_moments, (att_step, ATT * B))
            normalise(B - 1, moments2, rstd2, xhat2, ln2_rstd, ln2_xhat, ln2_h)
            assign(B - 1, choose(B - 1, False))

            dve.wait_ge(total_ps_ready, 1)
            step = Chain(dve, table_step, 0)
            step(nc.vector.tensor_tensor(count[:, :], misc[:, 0:E], region_at[:, :], ALU.subtract))
            step(nc.vector.tensor_scalar(count_i[:, :], count[:, :], float(TILE - 1), None, ALU.add))
            step(nc.vector.tensor_scalar(tiles_i[:, :], count_i[:, :], TILE.bit_length() - 1, None, ALU.arith_shift_right))
            step(nc.vector.tensor_copy(tiles_f[:, :], tiles_i[:, :]))
            step(nc.vector.tensor_copy(ends[:, 0:1], tiles_f[:, 0:1]))
            for e in range(1, E):
                step(nc.vector.tensor_tensor(ends[:, e:e + 1], ends[:, e - 1:e], tiles_f[:, e:e + 1], ALU.add))
            step(nc.vector.tensor_tensor(starts[:, :], ends[:, :], tiles_f[:, :], ALU.subtract))
            ends_b = ends[:, :].rearrange("p (o e) -> p o e", o=1).to_broadcast([P, ROW_TILES, E])
            tiles_b = tiles_f[:, :].rearrange("p (o e) -> p o e", o=1).to_broadcast([P, ROW_TILES, E])
            step(nc.vector.tensor_tensor(past[:, :, :], tile_no[:, :, :], ends_b, ALU.is_ge))
            step(nc.vector.tensor_reduce(tile_e[:, :], past[:, :, :], AX.X, ALU.add))
            step(nc.vector.tensor_tensor(past[:, :, :], past[:, :, :], tiles_b, ALU.mult))
            step(nc.vector.tensor_reduce(tile_s[:, :], past[:, :, :], AX.X, ALU.add))
            step(nc.vector.tensor_tensor(tile_s[:, :], tile_no[:, :, 0], tile_s[:, :], ALU.subtract))
            step(nc.vector.tensor_scalar(tile_u[:, :], tile_e[:, :], float(E), -float(TILE), ALU.is_lt, ALU.mult))
            step(nc.vector.tensor_tensor(tile_s[:, :], tile_s[:, :], tile_u[:, :], ALU.mult))
            step(nc.vector.scalar_tensor_tensor(out=tile_r[:, :], in0=tile_e[:, :], scalar=float(REGION), in1=tile_s[:, :],
                                                op0=ALU.mult, op1=ALU.subtract))
            step(nc.vector.tensor_copy(table_r[:, :], tile_r[:, :]), wait=False)
            step(nc.vector.tensor_scalar(table_e[:, :], tile_e[:, :], float(E - 1), None, ALU.min))
            nc.vector.tensor_tensor(pad_at[:, :], count[:, :], region_at[:, :], ALU.add).then_inc(table_ready, 1)

            def shared(n, b, half, par):
                dve.wait_ge(down_ready, n + 1)
                step = Chain(dve, y_step, 2 * n)
                bias = w_shared[:, B2_AT:PACK].rearrange("p (o d) -> p o d", o=1).to_broadcast([P, K, D])
                nc.vector.tensor_tensor(tile_y[par][:, :, :], yacc[par].rearrange("p (k d) -> p k d", k=K), bias, ALU.add).then_inc(y_evac, 1)
                dve.wait_ge(y_evac, n + 1)
                gate = mod[:, bass.ds(b, 1), 5, :].to_broadcast([P, K, D])
                step(nc.vector.tensor_tensor(tile_y[par][:, :, :], tile_y[par][:, :, :], gate, ALU.mult))
                r = res[:, bass.ds(b * G + K * half, K), :]
                step(nc.vector.tensor_tensor(r, r, tile_y[par][:, :, :], ALU.add))

            with dve.Fori(0, B) as b:
                for half in range(2):
                    shared(2 * b + half, b, half, half)

            def expert(j, i, par, first=False):
                dve.wait_ge(down_ready, SHARED_TILES + j + 1)
                if not first:
                    dve.wait_ge(y_sent[par], 16 * K * i)
                bias = w_exp[par][:, B2_AT:PACK].rearrange("p (o d) -> p o d", o=1).to_broadcast([P, K, D])
                nc.vector.tensor_tensor(tile_y[par][:, :, :], yacc[par].rearrange("p (k d) -> p k d", k=K), bias, ALU.add).then_inc(y_evac, 1)
                dve.wait_ge(y_evac, SHARED_TILES + j + 1)
                for k in range(K):
                    ins = nc.vector.tensor_scalar(tile_y[par][:, k, :], tile_y[par][:, k, :], tile_x[par][:, k, D + 1:D + 2], None, ALU.mult)
                ins.then_inc(y_ready, 1)

            for j in range(RING):
                expert(j, 0, j, True)
            with dve.Fori(1, ROW_TILES // RING) as i:
                for par in range(RING):
                    expert(RING * i + par, i, par)

            def combine(b, i, par):
                dve.wait_ge(z_loaded[par], 32 * (i + 1))
                step = Chain(dve, fin_step, 2 * b)
                z0, z1 = z_buf[par]
                gate = mod[:, bass.ds(b, 1), 5, :].to_broadcast([P, G, D])
                z0g = z0.rearrange("p (g d) -> p g d", d=D)
                step(nc.vector.tensor_tensor(z0, z0, z1, ALU.add))
                step(nc.vector.tensor_tensor(z0g, z0g, gate, ALU.mult))
                r = res[:, bass.ds(b * G, G), :]
                nc.vector.tensor_tensor(r, r, z0g, ALU.add).then_inc(fin_ready, 1)

            with dve.Fori(0, B // 2) as i:
                for par in range(2):
                    combine(2 * i + par, i, par)

        @block.tensor
        def _(pe):
            pe.wait_ge(loaded, 16 * N_LOADS)
            pe.wait_ge(silu_ready, 1)
            for n in range(2 * B):
                if n >= 4:
                    pe.wait_ge(mod_evac, n - 3)
                half = (n % 2) * (MOD // 2)
                nc.tensor.matmul(score[:, n % 4, 0:MOD // 2], silu_b[:, n // 2, :], wmod_sb[:, half:half + MOD // 2],
                                 start=True, stop=True).then_inc(mod_ps_ready, 1)
            pe.wait_ge(mod_evac, 2 * B)
            pe.wait_ge(const_ready, 1)

            def misc_rows(src, half):
                for k in range(4):
                    ins = nc.tensor.transpose(misc[:, k * P:(k + 1) * P], src(4 * half + k), ident[:, :])
                return ins

            def transpose_h(b, half, first):
                pe.wait_ge(ln1_h, b + 1)
                if half or not first:
                    pe.wait_ge(qt_ready if not half else ht_ready, 2 * b + half)
                misc_rows(lambda g: h_sb[:, g, :], half).then_inc(ht_ps_ready, 1)

            def queries(b):
                for half in range(2):
                    pe.wait_ge(ht_ready, 2 * b + 2)
                    if half:
                        pe.wait_ge(qt_ready, 2 * b + 1)
                    nc.tensor.matmul(misc[:, :], watt_sb[:, :], h_t[:, half * 512:half * 512 + 512],
                                     start=True, stop=True).then_inc(qt_ps_ready, 1)

            def scores(b, t, first):
                if t == 0:
                    pe.wait_ge(qt_ready, 2 * b + 2)
                if not (first and t < 2):
                    pe.wait_ge(score_used, G * b + t - 1)
                for half in range(2):
                    ins = nc.tensor.matmul(score[:, 2 * (t % 2) + half, :], h_t[:, t * P:(t + 1) * P],
                                           q_t[:, half * 512:half * 512 + 512], start=True, stop=True)
                ins.then_inc(score_ready, 1)

            def values(b, t, first):
                pe.wait_ge(prob_ready, G * b + t + 1)
                if t == 0:
                    pe.wait_ge(values_ready, b + 1)
                    if not first:
                        pe.wait_ge(value_used, b)
                for s in range(G):
                    c0 = (s % 3) * (D + 1)
                    ins = nc.tensor.matmul(value[:, s // 3, c0:c0 + D + 1], prob[:, t % 4, s * P:(s + 1) * P],
                                           h_ones[:, bass.ds(b % 2, 1), t, :].rearrange("p o d -> p (o d)"),
                                           start=(t == 0 and s % 3 == 0), stop=(t == G - 1), skip_group_check=True)
                ins.then_inc(value_step, 1)

            def transpose_h2(b, half):
                pe.wait_ge(ln2_h, b + 1)
                if half:
                    pe.wait_ge(h2t_staged, 2 * b + 1)
                misc_rows(lambda g: row_1[:, g, 0:D], half).then_inc(h2t_ps_ready, 1)

            def gate_logits(b):
                pe.wait_ge(h2t_staged, 2 * b + 2)
                for g in range(G):
                    ins = nc.tensor.matmul(misc[:, g * E:(g + 1) * E], h2_ts[:, g * P:(g + 1) * P], wg_sb[:, :], start=True, stop=True)
                ins.then_inc(logits_ps_ready, 1)

            def ranks(b):
                pe.wait_ge(chosen_ready, b + 1)
                nc.tensor.matmul(misc[:, 0:E], before[:, :], earlier[:, G, :], start=True, stop=False)
                nc.tensor.matmul(misc[:, 0:E], ones[:, :], carry[:, :], start=False, stop=True).then_inc(rank_ps_ready, 1)

            def batch(b, first=False, second=False, last=False):
                for t in range(G):
                    scores(b, t, first)
                    if t >= 2:
                        values(b, t - 2, first)
                    if t == 4 and not first:
                        transpose_h2(b - 1, 0)
                        transpose_h2(b - 1, 1)
                    if t == 5 and not first:
                        gate_logits(b - 1)
                    if t == 6 and not first:
                        ranks(b - 1)
                values(b, G - 2, first)
                if not last:
                    if not first:
                        pe.wait_ge(rank_used, b)
                    transpose_h(b + 1, 0, False)
                    transpose_h(b + 1, 1, False)
                    queries(b + 1)
                values(b, G - 1, first)

            transpose_h(0, 0, True)
            transpose_h(0, 1, True)
            queries(0)
            batch(0, first=True)
            batch(1, second=True)
            with pe.Fori(2, B - 1) as b:
                batch(b)
            batch(B - 1, last=True)
            pe.wait_ge(rank_used, B - 1)
            transpose_h2(B - 1, 0)
            transpose_h2(B - 1, 1)
            gate_logits(B - 1)
            ranks(B - 1)
            pe.wait_ge(slots_ready, B)
            nc.tensor.matmul(misc[:, 0:E], ones[:, :], carry[:, :], start=True, stop=True).then_inc(total_ps_ready, 1)

            def up(n, w, src, first=False):
                for c in range(C):
                    if not first:
                        pe.wait_ge(hidden_ready, C * (n - 1) + c + 1)
                    nc.tensor.matmul(score[:, c, :], w[:, c * P:(c + 1) * P], src, start=True, stop=True).then_inc(up_ready, 1)

            def down(n, w, par, first=False):
                if not first:
                    pe.wait_ge(y_evac, n - 1)
                for c in range(C):
                    pe.wait_ge(hidden_ready, C * n + c + 1)
                    for k in range(K):
                        ins = nc.tensor.matmul(yacc[par][:, k * D:(k + 1) * D], hidden[par][:, c, k * P:(k + 1) * P],
                                               w[:, W2_AT + c * D:W2_AT + (c + 1) * D],
                                               start=(c == 0 and k == 0), stop=(c == C - 1), skip_group_check=True)
                ins.then_inc(down_ready, 1)

            pe.wait_ge(h2t_kept, B)
            pe.wait_ge(value_used, B)
            for n in range(2):
                up(n, w_shared, h2_t[:, n * TILE:(n + 1) * TILE], first=(n == 0))
                down(n, w_shared, n, first=True)
            with pe.Fori(1, SHARED_TILES // 2) as i:
                for par in range(2):
                    n = 2 * i + par
                    up(n, w_shared, h2_t[:, bass.ds(n * TILE, TILE)])
                    down(n, w_shared, par)

            def transpose_rows(j, i, par, first=False):
                pe.wait_ge(x_loaded[par], 16 * (i + 1))
                if not first:
                    pe.wait_ge(xt_ready, j)
                for k in range(K):
                    ins = nc.tensor.transpose(xt_ps[:, k * P:(k + 1) * P], tile_x[par][:, k, 0:D], ident[:, :])
                ins.then_inc(xt_ps_ready, 1)

            def expert_up(j, i, par):
                pe.wait_ge(xt_ready, j + 1)
                pe.wait_ge(w_loaded[par], 16 * (i + 1))
                up(SHARED_TILES + j, w_exp[par], tile_xt[:, :])

            transpose_rows(0, 0, 0, True)

            def expert(i, par, last=False):
                j = RING * i + par
                expert_up(j, i, par)
                if not last:
                    transpose_rows(j + 1, i + (par + 1) // RING, (par + 1) % RING)
                down(SHARED_TILES + j, w_exp[par], par)

            with pe.Fori(0, ROW_TILES // RING - 1) as i:
                for par in range(RING):
                    expert(i, par)
            for par in range(RING):
                expert(ROW_TILES // RING - 1, par, last=(par == RING - 1))


def kernel(**inputs):
    from concourse import bacc
    from concourse.bass_utils import run_bass_kernel_spmd

    a = {k.removeprefix("L0_"): np.asarray(v) for k, v in inputs.items()}

    def chunks(w):
        return w.reshape(C, P, D).transpose(1, 0, 2).reshape(P, C * D)

    def pack(w1, b1, w2, b2):
        return np.concatenate([w1, chunks(w2), b1.reshape(C, P).T, np.broadcast_to(b2, (P, D))], axis=1)

    packs = [pack(a["ffn_W1"][e], a["ffn_b1"][e], a["ffn_W2"][e], a["ffn_b2"][e]) for e in range(E)]
    packs.append(pack(a["ffn_Ws1"], a["ffn_bs1"], a["ffn_Ws2"], a["ffn_bs2"]))
    arrays = {
        "x": a["attn_x"].reshape(T, D), "c_t": a["c"].T, "wmod": a["wmod"], "w_att": a["attn_W"],
        "b_att": a["attn_b"].reshape(D, 1), "wg": a["ffn_Wg"], "packs": np.stack(packs),
    }
    arrays = {k: np.ascontiguousarray(v) for k, v in arrays.items()}
    nc = bacc.Bacc("TRN2", target_bir_lowering=False, num_devices=1)
    args = [nc.dram_tensor(k, v.shape, mybir.dt.from_np(v.dtype), kind="ExternalInput").ap() for k, v in arrays.items()]
    args.append(nc.dram_tensor("out", (T, D), F32, kind="ExternalOutput").ap())
    adaln_moe(nc, *args)
    r = run_bass_kernel_spmd(nc, [arrays], core_ids=[0])
    return r.results[0]["out"].reshape(B, S, D)
```

```python
from contextlib import ExitStack

import numpy as np

import concourse.bass as bass
from concourse import mybir

F32 = mybir.dt.float32
I32 = mybir.dt.int32
U32 = mybir.dt.uint32
ALU = mybir.AluOpType
ACT = mybir.ActivationFunctionType
AX = mybir.AxisListType

P = 128
B, S, D = 8, 1024, 128
G = S // P
T = B * S
E, F = 8, 512
C = F // P
TILE = 512
K = TILE // P
REGION = T + TILE
ROW = D + 2
ROW_TILES = 2 * T // TILE + E - 1
SPARE = E * REGION
X_ROWS = SPARE + TILE
Z_ROWS = 2 * T
NOWHERE = 2 * Z_ROWS
W2_AT, B1_AT, B2_AT = F, F + C * D, F + C * D + C
PACK = B2_AT + D
MOD = 6 * D
EPS_ATT = 1e-7
EPS_LN = 1e-5
SHARED_TILES = T // TILE
FRONT = 8
RING = 3
assert ROW_TILES % RING == 0


class Chain:

    def __init__(self, eng, sem, start):
        self.eng, self.sem, self.start, self.n = eng, sem, start, 0

    def __call__(self, ins, wait=True):
        ins.then_inc(self.sem, 1)
        self.n += 1
        if wait:
            self.eng.wait_ge(self.sem, self.now())

    def now(self):
        return self.start + self.n


def adaln_moe(nc, x, c_t, wmod, w_att, b_att, wg, packs, out):
    with ExitStack() as ctx:
        def sb(name, shape, dt=F32):
            return ctx.enter_context(nc.sbuf_tensor(name, shape, dt))

        def ps(name, shape):
            return ctx.enter_context(nc.psum_tensor(name, shape, F32))

        def sem(name):
            return ctx.enter_context(nc.semaphore(name))

        rows_x = nc.dram_tensor("rows_x", [X_ROWS, ROW], F32).ap()
        rows_z = nc.dram_tensor("rows_z", [Z_ROWS, D], F32).ap()

        ident = sb("ident", [P, P])
        offdiag = sb("offdiag", [P, P])
        before = sb("before", [P, P])
        ones = sb("ones", [P, P])
        lw = sb("lw", [P, (2 * G - 1) * P])
        minus_half = sb("minus_half", [P, B * G])
        expert_no = sb("expert_no", [P, G, E])
        token_no = sb("token_no", [P, G])
        region_at = sb("region_at", [P, E])
        tile_no = sb("tile_no", [P, ROW_TILES, E])
        pad_rows = sb("pad_rows", [P, K, ROW])
        c_sb = sb("c_sb", [P, B])
        silu = sb("silu", [P, B])
        wmod_sb = sb("wmod_sb", [P, MOD])
        watt_sb = sb("watt_sb", [D, D])
        batt_sb = sb("batt_sb", [D, 1])
        wg_sb = sb("wg_sb", [D, E])
        w_shared = sb("w_shared", [P, PACK])
        w_exp = [sb(f"w_exp{i}", [P, PACK]) for i in range(RING)]
        mod = sb("mod", [P, B, 6, D])
        mod_col = sb("mod_col", [D, 4, B])
        res = sb("res", [P, B * G, D])
        h2_t = sb("h2_t", [D, T])
        lw_mask = h2_t[:, 0:(2 * G - 1) * P]
        stats = sb("stats", [P, G, 6])
        moments = sb("moments", [P, B * G, 2])
        rstd = sb("rstd", [P, B * G])
        shift = sb("shift", [P, B * G])
        stats2 = sb("stats2", [P, G, 6])
        moments2 = sb("moments2", [P, G, 2])
        rstd2 = sb("rstd2", [P, G])
        xhat = sb("xhat", [P, G, D])
        xhat2 = sb("xhat2", [P, G, D])
        res_tmp = sb("res_tmp", [P, G, D])
        silu_b = res_tmp
        half_sign = xhat2
        h_ones = sb("h_ones", [P, 2, G, D + 1])
        work = sb("work", [P, RING * C * TILE])
        prob = work[:, 0:4 * S].rearrange("p (t s) -> p t s", t=4)
        h_t = [work[:, 4 * S:5 * S], work[:, 5 * S:6 * S]]
        q_t = [sb(f"q_t{i}", [D, S]) for i in range(2)]
        den = sb("den", [P, G])
        rden = sb("rden", [P, G])
        row_1 = sb("row_1", [P, G, ROW])
        row_2 = sb("row_2", [P, G, ROW])
        h2_ts = sb("h2_ts", [D, S])
        logits = sb("logits", [P, G, E])
        top_v = sb("top_v", [P, G, E])
        top_i = sb("top_i", [P, G, E], U32)
        top_f = sb("top_f", [P, G, E])
        hot_1 = sb("hot_1", [P, G, E])
        hot_2 = sb("hot_2", [P, G, E])
        chosen = sb("chosen", [P, G, E])
        earlier = sb("earlier", [P, G + 1, E])
        carry = sb("carry", [P, E])
        place = sb("place", [P, G, E])
        slot_f = sb("slot_f", [P, 2, G])
        slot = sb("slot", [P, 2, G], I32)
        gap = sb("gap", [P, G])
        gap_e = sb("gap_e", [P, G])
        gap_1 = sb("gap_1", [P, G])
        w_first = sb("w_first", [P, G])
        w_second = sb("w_second", [P, G])
        count = sb("count", [P, E])
        count_i = sb("count_i", [P, E], I32)
        tiles_i = sb("tiles_i", [P, E], I32)
        tiles_f = sb("tiles_f", [P, E])
        ends = sb("ends", [P, E])
        starts = sb("starts", [P, E])
        past = sb("past", [P, ROW_TILES, E])
        tile_e = sb("tile_e", [P, ROW_TILES])
        tile_s = sb("tile_s", [P, ROW_TILES])
        tile_u = sb("tile_u", [P, ROW_TILES])
        tile_r = sb("tile_r", [P, ROW_TILES])
        table_e = sb("table_e", [P, ROW_TILES], I32)
        table_r = sb("table_r", [P, ROW_TILES], I32)
        pad_at = sb("pad_at", [P, E], I32)
        tile_x = [sb(f"tile_x{i}", [P, K, ROW]) for i in range(RING)]
        tile_xt = res_tmp[:, 0:K, :].rearrange("p k d -> p (k d)")
        hidden = [work[:, i * C * TILE:(i + 1) * C * TILE].rearrange("p (c n) -> p c n", c=C) for i in range(RING)]
        tile_y = [sb(f"tile_y{i}", [P, K, D]) for i in range(RING)]

        score = ps("score", [P, 4, 512])
        value = ps("value", [P, 3, 512])
        misc = ps("misc", [P, 512])
        yacc = [value[:, 0, :], value[:, 1, :], misc[:, :]]
        xt_ps = value[:, 2, :]

        def value_at(s):
            return value[:, s // 3, (s % 3) * (D + 1):(s % 3) * (D + 1) + D]

        cond_loaded = sem("cond_loaded")
        small_loaded = sem("small_loaded")
        x_in = [sem(f"x_in{i}") for i in range(3)]
        shared_loaded = sem("shared_loaded")
        const_ready = sem("const_ready")
        const_step = sem("const_step")
        places_passed = sem("places_passed")
        distance_ready = sem("distance_ready")
        silu_step = sem("silu_step")
        lw_step = sem("lw_step")
        silu_exp = sem("silu_exp")
        silu_ready = sem("silu_ready")
        col_ps_ready = sem("col_ps_ready")
        col_ready = sem("col_ready")
        mod_ps_ready = sem("mod_ps_ready")
        mod_evac = sem("mod_evac")
        mod_step = sem("mod_step")

        ln1_step = sem("ln1_step")
        ln1_moments = sem("ln1_moments")
        ln1_pool_step = sem("ln1_pool_step")
        ln1_rstd = sem("ln1_rstd")
        ln1_ready = sem("ln1_ready")
        ln1_xhat = sem("ln1_xhat")
        gate_step = sem("gate_step")
        gated = sem("gated")
        ht_ps_ready = sem("ht_ps_ready")
        ht_ready = sem("ht_ready")
        qt_ps_ready = sem("qt_ps_ready")
        qt_ready = sem("qt_ready")
        score_ready = sem("score_ready")
        score_used = sem("score_used")
        tanh_done = sem("tanh_done")
        exp_done = sem("exp_done")
        prob_ready = sem("prob_ready")
        value_step = sem("value_step")
        value_used = sem("value_used")
        att_step = sem("att_step")
        rden_ready = sem("rden_ready")
        ln2_step = sem("ln2_step")
        ln2_moments = sem("ln2_moments")
        ln2_pool_step = sem("ln2_pool_step")
        ln2_rstd = sem("ln2_rstd")
        ln2_xhat = sem("ln2_xhat")
        ln2_mod_step = sem("ln2_mod_step")
        ln2_h = sem("ln2_h")
        second_rows = sem("second_rows")
        h2t_ps_ready = sem("h2t_ps_ready")
        h2t_staged = sem("h2t_staged")
        h2t_kept = sem("h2t_kept")
        logits_ps_ready = sem("logits_ps_ready")
        logits_ready = sem("logits_ready")
        route_step = sem("route_step")
        chosen_ready = sem("chosen_ready")
        gap_ready = sem("gap_ready")
        gap_exp = sem("gap_exp")
        rank_ps_ready = sem("rank_ps_ready")
        rank_used = sem("rank_used")
        slots_ready = sem("slots_ready")
        scattered = sem("scattered")

        total_ps_ready = sem("total_ps_ready")
        table_step = sem("table_step")
        table_ready = sem("table_ready")
        padded = sem("padded")
        x_loaded = [sem(f"x_loaded{i}") for i in range(RING)]
        w_loaded = [sem(f"w_loaded{i}") for i in range(RING)]
        xt_ps_ready = sem("xt_ps_ready")
        xt_ready = sem("xt_ready")
        up_ready = sem("up_ready")
        hidden_ready = sem("hidden_ready")
        down_ready = sem("down_ready")
        y_evac = sem("y_evac")
        y_step = sem("y_step")
        y_ready = sem("y_ready")
        y_sent = [sem(f"y_sent{i}") for i in range(RING)]
        z_loaded = [sem(f"z_loaded{i}") for i in range(2)]
        fin_step = sem("fin_step")
        fin_ready = sem("fin_ready")
        front_loaded = sem("front_loaded")
        front_step = sem("front_step")
        front_stored = sem("front_stored")
        stored = sem("stored")

        x_v = x.rearrange("(b p g) d -> p b (g d)", b=B, p=P, g=G)
        out_v = out.rearrange("(b p g) d -> b p (g d)", b=B, p=P, g=G)
        z_v = rows_z.rearrange("(k b p g) d -> k b p (g d)", k=2, b=B, p=P, g=G)
        ROUTE, CHOOSE = 26, 13

        z_half = [[hidden[2][:, 2 * i + k, :] for k in range(2)] for i in range(2)]
        z_front = [xhat[:, :, :], xhat2[:, :, :]]

        block = ctx.enter_context(nc.Block())

        def wait(eng, on, count):
            if not isinstance(count, int) or count > 0:
                eng.wait_ge(on, count)

        def exists(b):
            return not isinstance(b, int) or 0 <= b < B

        def batches(eng, batch):
            batch(0, 0)
            batch(1, 1)
            with eng.Fori(1, B // 2 - 1) as i:
                for par in range(2):
                    batch(2 * i + par, par)
            batch(B - 2, 0)
            batch(B - 1, 1)

        def wait_alone(eng, *waits):
            for on, v in waits:
                if not isinstance(v, int) or v > 0:
                    eng.wait_ge(on, v)
                    eng.sem_inc(places_passed, 1)

        @block.sync
        def _(sp):
            for b in range(B):
                sp.dma_start(res[:, b * G:(b + 1) * G, :].rearrange("p g d -> p (g d)"), x_v[:, b, :]).then_inc(x_in[min(b, 2)], 16)
            sp.dma_start(w_shared[:, :], packs[E]).then_inc(shared_loaded, 16)

            sp.wait_ge(table_ready, 1)
            sp.wait_ge(scattered, 16 * 2 * G * B)
            sp.wait_ge(const_ready, 1)
            for e in range(E):
                at = sp.value_load(pad_at[0:1, e:e + 1], min_val=0, max_val=SPARE - TILE)
                sp.dma_start(rows_x[bass.ds(at, TILE), :].rearrange("(p k) r -> p (k r)", p=P),
                             pad_rows[:, :, :].rearrange("p k r -> p (k r)")).then_inc(padded, 16)
            sp.dma_start(rows_x[SPARE:X_ROWS, :].rearrange("(p k) r -> p (k r)", p=P),
                         pad_rows[:, :, :].rearrange("p k r -> p (k r)")).then_inc(padded, 16)
            sp.wait_ge(padded, 16 * (E + 1))

            def load_tile(j, i, par, first):
                if not first:
                    wait_alone(sp, (y_sent[par], 16 * K * i), (y_evac, FRONT + j - RING + 1))
                e = sp.value_load(table_e[0:1, bass.ds(j, 1)], min_val=0, max_val=E - 1)
                r = sp.value_load(table_r[0:1, bass.ds(j, 1)], min_val=0, max_val=SPARE)
                sp.dma_start(tile_x[par][:, :, :].rearrange("p k r -> p (k r)"),
                             rows_x[bass.ds(r, TILE), :].rearrange("(p k) r -> p (k r)", p=P)).then_inc(x_loaded[par], 16)
                sp.dma_start(w_exp[par][:, :], packs[bass.ds(e, 1), :, :].rearrange("e p n -> (e p) n")).then_inc(w_loaded[par], 16)

            for par in range(RING):
                load_tile(par, 0, par, True)
            with sp.Fori(1, ROW_TILES // RING) as i:
                for par in range(RING):
                    load_tile(RING * i + par, i, par, False)

            for par in range(RING):
                sp.wait_ge(y_sent[par], 16 * K * (ROW_TILES // RING))

            def load_results(b, half):
                for k in range(2):
                    sp.dma_start(z_half[half][k], z_v[k, bass.ds(b, 1), :, half * TILE:(half + 1) * TILE]
                                 .rearrange("b p n -> (b p) n")).then_inc(z_loaded[half], 16)

            def store(b, half):
                sp.wait_ge(fin_ready, 2 * b + half + 1 - FRONT)
                sp.dma_start(out_v[bass.ds(b, 1), :, half * TILE:(half + 1) * TILE].rearrange("b p n -> (b p) n"),
                             res[:, bass.ds(b * G + K * half, K), :].rearrange("p g d -> p (g d)")).then_inc(stored, 16)

            for half in range(2):
                load_results(FRONT // 2, half)
            with sp.Fori(FRONT // 2, B - 1) as b:
                for half in range(2):
                    store(b, half)
                    load_results(b + 1, half)
            for half in range(2):
                store(B - 1, half)
            sp.wait_ge(stored, 16 * (SHARED_TILES - FRONT))

        @block.gpsimd
        def _(pool):
            step = Chain(pool, const_step, 0)
            nc.gpsimd.iota(lw_mask[:, :].rearrange("p (g q) -> p g q", q=P), pattern=[[1, 2 * G - 1], [G, P]],
                           base=-(G - 1), channel_multiplier=-G, allow_small_or_imprecise_dtypes=True).then_inc(distance_ready, 1)
            step(nc.gpsimd.memset(minus_half[:, :], -0.5), wait=False)
            step(nc.gpsimd.memset(ident[:, :], 0.0), wait=False)
            step(nc.gpsimd.memset(offdiag[:, :], 1.0), wait=False)
            step(nc.gpsimd.memset(before[:, :], 1.0), wait=False)
            step(nc.gpsimd.memset(pad_rows[:, :, :], 0.0))
            step(nc.gpsimd.affine_select(out=ident[:, :], in_=ident[:, :], compare_op=ALU.not_equal, fill=1.0,
                                         base=0, pattern=[[-1, P]], channel_multiplier=1), wait=False)
            step(nc.gpsimd.affine_select(out=offdiag[:, :], in_=offdiag[:, :], compare_op=ALU.not_equal, fill=0.0,
                                         base=0, pattern=[[-1, P]], channel_multiplier=1), wait=False)
            step(nc.gpsimd.affine_select(out=before[:, :], in_=before[:, :], compare_op=ALU.is_gt, fill=0.0,
                                         base=0, pattern=[[1, P]], channel_multiplier=-1), wait=False)
            step(nc.gpsimd.memset(ones[:, :], 1.0), wait=False)
            step(nc.gpsimd.memset(h_ones[:, :, :, D:D + 1], 1.0), wait=False)
            step(nc.gpsimd.memset(carry[:, :], 0.0), wait=False)
            step(nc.gpsimd.memset(earlier[:, 0, :], 0.0), wait=False)
            step(nc.gpsimd.iota(expert_no[:, :, :], pattern=[[0, G], [1, E]], base=0, channel_multiplier=0,
                                allow_small_or_imprecise_dtypes=True), wait=False)
            step(nc.gpsimd.iota(token_no[:, :], pattern=[[1, G]], base=0, channel_multiplier=G,
                                allow_small_or_imprecise_dtypes=True), wait=False)
            step(nc.gpsimd.iota(region_at[:, :], pattern=[[REGION, E]], base=0, channel_multiplier=0,
                                allow_small_or_imprecise_dtypes=True), wait=False)
            step(nc.gpsimd.iota(tile_no[:, :, :], pattern=[[1, ROW_TILES], [0, E]], base=0, channel_multiplier=0,
                                allow_small_or_imprecise_dtypes=True), wait=False)
            step(nc.gpsimd.iota(pad_rows[:, :, D:D + 1].bitcast(I32), pattern=[[0, K]], base=NOWHERE, channel_multiplier=0))
            nc.gpsimd.tensor_copy(carry[0:1, :], region_at[0:1, :]).then_inc(const_ready, 1)

            def rstd_1(b0, b1):
                pool.wait_ge(ln1_moments, b1)
                step = Chain(pool, ln1_pool_step, b0)
                rs = rstd[:, b0 * G:b1 * G]
                nc.gpsimd.tensor_scalar(rs, moments[:, b0 * G:b1 * G, 1], EPS_LN, None, ALU.add).then_inc(ln1_pool_step, b1 - b0)
                pool.wait_ge(ln1_pool_step, b1)
                nc.gpsimd.tensor_tensor(rs, rs, minus_half[:, 0:(b1 - b0) * G], ALU.pow).then_inc(ln1_rstd, b1 - b0)

            def modulation(b0, b1, start):
                pool.wait_ge(mod_evac, 2 * b1)
                step = Chain(pool, mod_step, start)
                for at in (0, 3):
                    shift_, scale, gate = (mod[:, b0:b1, at + i, :] for i in range(3))
                    sz = half_sign[:, b0:b1, :]
                    step(nc.gpsimd.tensor_scalar(scale, scale, 1.0, None, ALU.add), wait=False)
                    step(nc.gpsimd.tensor_scalar(sz, gate, 0.0, -0.5, ALU.is_ge, ALU.add))
                    step(nc.gpsimd.tensor_tensor(gate, gate, sz, ALU.mult))
                    step(nc.gpsimd.tensor_scalar(gate, gate, 0.125, 4.0, ALU.max, ALU.mult))
                    step(nc.gpsimd.tensor_tensor(gate, gate, sz, ALU.mult))
                    if at == 0:
                        step(nc.gpsimd.tensor_tensor(scale, scale, gate, ALU.mult), wait=False)
                        step(nc.gpsimd.tensor_tensor(shift_, shift_, gate, ALU.mult))
                return start + step.n

            def gate_rows(b, par):
                pool.wait_ge(ln1_xhat, b + 1)
                wait(pool, value_step, G * (b - 1))
                h = h_ones[:, par, :, 0:D]
                scale = mod[:, bass.ds(b, 1), 1, :].to_broadcast([P, G, D])
                shift_ = mod[:, bass.ds(b, 1), 0, :].to_broadcast([P, G, D])
                nc.gpsimd.tensor_tensor(h, xhat[:, :, :], scale, ALU.mult).then_inc(gate_step, 1)
                pool.wait_ge(gate_step, b + 1)
                nc.gpsimd.tensor_tensor(h, h, shift_, ALU.add).then_inc(gated, 1)

            def rstd_2(b):
                wait_alone(pool, (ln2_moments, b + 1))
                nc.gpsimd.tensor_scalar(rstd2[:, :], moments2[:, :, 1], EPS_LN, None, ALU.add).then_inc(ln2_pool_step, 1)
                pool.wait_ge(ln2_pool_step, b + 1)
                nc.gpsimd.tensor_tensor(rstd2[:, :], rstd2[:, :], minus_half[:, 0:G], ALU.pow).then_inc(ln2_rstd, 1)

            def expert_rows(b):
                pool.wait_ge(ln2_xhat, b + 1)
                pool.wait_ge(h2t_ps_ready, 2 * b + 2)
                wait(pool, scattered, 16 * 2 * G * b)
                wait(pool, second_rows, b)
                scale = mod[:, bass.ds(b, 1), 4, :].to_broadcast([P, G, D])
                shift_ = mod[:, bass.ds(b, 1), 3, :].to_broadcast([P, G, D])
                nc.gpsimd.tensor_tensor(xhat2[:, :, :], xhat2[:, :, :], scale, ALU.mult).then_inc(ln2_mod_step, 1)
                pool.wait_ge(ln2_mod_step, b + 1)
                nc.gpsimd.tensor_tensor(row_1[:, :, 0:D], xhat2[:, :, :], shift_, ALU.add).then_inc(ln2_h, 1)

            def scatter(b):
                wait_alone(pool, (slots_ready, b + 1))
                for k, rows in enumerate((row_1, row_2)):
                    if k == 1:
                        wait_alone(pool, (second_rows, b + 1))
                    for g in range(G):
                        nc.gpsimd.indirect_dma_start(rows_x[:, :], bass.IndirectOffsetOnAxis(ap=slot[:, k, g:g + 1], axis=0),
                                                     rows[:, g, :], None).then_inc(scattered, 16)

            def batch(b, par):
                if exists(b + 1):
                    gate_rows(b + 1, 1 - par)
                if exists(b - 2):
                    expert_rows(b - 2)
                if exists(b - 1):
                    rstd_2(b - 1)
                if exists(b - 2):
                    scatter(b - 2)

            rstd_1(0, 1)
            done = modulation(0, 1, 0)
            rstd_1(1, 2)
            gate_rows(0, 0)
            done = modulation(1, B, done)
            rstd_1(2, B)
            batches(pool, batch)
            expert_rows(B - 2)
            rstd_2(B - 1)
            scatter(B - 2)
            expert_rows(B - 1)
            scatter(B - 1)

            def send(j, par):
                wait_alone(pool, (y_ready, j + 1))
                for k in range(K):
                    nc.gpsimd.indirect_dma_start(rows_z[:, :], bass.IndirectOffsetOnAxis(ap=tile_x[par][:, k, D:D + 1].bitcast(I32), axis=0),
                                                 tile_y[par][:, k, :], None, bounds_check=Z_ROWS - 1, oob_is_err=False).then_inc(y_sent[par], 16)

            with pool.Fori(0, ROW_TILES // RING) as i:
                for par in range(RING):
                    send(RING * i + par, par)

            for par in range(RING):
                pool.wait_ge(y_sent[par], 16 * K * (ROW_TILES // RING))
            pool.wait_ge(y_evac, FRONT)
            with pool.Fori(0, FRONT // 2) as b:
                for k in range(2):
                    nc.gpsimd.dma_start(z_front[k].rearrange("p g d -> p (g d)"),
                                        z_v[k, bass.ds(b, 1), :, :].rearrange("b p n -> (b p) n")).then_inc(front_loaded, 16)
                pool.wait_ge(front_loaded, 32 * (b + 1))
                step = Chain(pool, front_step, 3 * b)
                gate = mod[:, bass.ds(b, 1), 5, :].to_broadcast([P, G, D])
                r = res[:, bass.ds(b * G, G), :]
                step(nc.gpsimd.tensor_tensor(z_front[0], z_front[0], z_front[1], ALU.add))
                step(nc.gpsimd.tensor_tensor(z_front[0], z_front[0], gate, ALU.mult))
                step(nc.gpsimd.tensor_tensor(r, r, z_front[0], ALU.add), wait=False)
                wait_alone(pool, (front_step, step.now()))
                nc.gpsimd.dma_start(out_v[bass.ds(b, 1), :, :].rearrange("b p n -> (b p) n"),
                                    r.rearrange("p g d -> p (g d)")).then_inc(front_stored, 16)
            pool.wait_ge(front_stored, 16 * (FRONT // 2))

        @block.scalar
        def _(act):
            act.dma_start(c_sb[:, :], c_t).then_inc(cond_loaded, 16)
            act.dma_start(wmod_sb[:, :], wmod).then_inc(cond_loaded, 16)
            act.dma_start(watt_sb[:, :], w_att).then_inc(small_loaded, 16)
            act.dma_start(batt_sb[:, :], b_att).then_inc(small_loaded, 16)
            act.dma_start(wg_sb[:, :], wg).then_inc(small_loaded, 16)
            act.wait_ge(cond_loaded, 32)
            nc.scalar.activation(silu[:, :], c_sb[:, :], ACT.Exp, scale=-1.0).then_inc(silu_exp, 1)

            def modulation(n0, n1):
                for n in range(n0, n1):
                    act.wait_ge(mod_ps_ready, n + 1)
                    nc.scalar.activation(mod[:, n // 2, 3 * (n % 2):3 * (n % 2) + 3, :].rearrange("p m d -> p (m d)"),
                                         score[:, n % 4, 0:MOD // 2], ACT.Copy).then_inc(mod_evac, 1)

            def normalise(b):
                act.wait_ge(ln1_ready, b + 1)
                wait(act, ht_ps_ready, 2 * b)
                wait_alone(act, (gated, b))
                for g in range(G):
                    at = b * G + g
                    ins = nc.scalar.activation(xhat[:, g, :], res[:, bass.ds(at, 1), :].rearrange("p o d -> p (o d)"), ACT.Identity,
                                               scale=rstd[:, bass.ds(at, 1)], bias=shift[:, bass.ds(at, 1)])
                ins.then_inc(ln1_xhat, 1)

            def transposed(b, par, half):
                wait_alone(act, (ht_ps_ready, 2 * b + half + 1))
                nc.scalar.activation(h_t[par][:, half * 512:half * 512 + 512], misc[:, :], ACT.Identity,
                                     scale=mod_col[:, 2, bass.ds(b, 1)], bias=mod_col[:, 0, bass.ds(b, 1)]).then_inc(ht_ready, 1)

            def queries(b, par, half):
                act.wait_ge(qt_ps_ready, 2 * b + half + 1)
                nc.scalar.activation(q_t[par][:, half * 512:half * 512 + 512], misc[:, :], ACT.Identity,
                                     bias=batt_sb[:, 0:1]).then_inc(qt_ready, 1)

            def weights(b, t):
                act.wait_ge(score_used, G * b + t + 1)
                nc.scalar.activation(prob[:, t % 4, :], prob[:, t % 4, :], ACT.Tanh).then_inc(tanh_done, 1)
                act.wait_ge(tanh_done, G * b + t + 1)
                nc.scalar.activation(prob[:, t % 4, :], prob[:, t % 4, :], ACT.Exp).then_inc(exp_done, 1)

            def second_copy(b):
                act.wait_ge(ln2_h, b + 1)
                nc.scalar.activation(row_2[:, :, 0:D], row_1[:, :, 0:D], ACT.Copy).then_inc(second_rows, 1)

            def stage_h2t(b, half):
                wait(act, logits_ps_ready, b)
                wait(act, h2t_kept, b)
                wait_alone(act, (h2t_ps_ready, 2 * b + half + 1))
                nc.scalar.activation(h2_ts[:, half * 512:half * 512 + 512], misc[:, :], ACT.Identity,
                                     scale=mod_col[:, 3, bass.ds(b, 1)], bias=mod_col[:, 1, bass.ds(b, 1)]).then_inc(h2t_staged, 1)

            def keep_h2t(b):
                wait_alone(act, (h2t_staged, 2 * b + 2))
                nc.scalar.activation(h2_t[:, bass.ds(b * S, S)], h2_ts[:, :], ACT.Copy).then_inc(h2t_kept, 1)

            def gap_exponent(b):
                act.wait_ge(gap_ready, b + 1)
                nc.scalar.activation(gap_e[:, :], gap[:, :], ACT.Exp).then_inc(gap_exp, 1)

            def batch(b, par):
                weights(b, 0)
                if exists(b - 2):
                    keep_h2t(b - 2)
                if exists(b + 1):
                    normalise(b + 1)
                weights(b, 1)
                if exists(b - 2):
                    gap_exponent(b - 2)
                weights(b, 2)
                weights(b, 3)
                if exists(b + 1):
                    transposed(b + 1, 1 - par, 0)
                weights(b, 4)
                if exists(b + 1):
                    transposed(b + 1, 1 - par, 1)
                if exists(b - 2):
                    second_copy(b - 2)
                weights(b, 5)
                if exists(b + 1):
                    queries(b + 1, 1 - par, 0)
                weights(b, 6)
                if exists(b + 1):
                    queries(b + 1, 1 - par, 1)
                if exists(b - 1):
                    stage_h2t(b - 1, 0)
                weights(b, 7)
                if exists(b - 1):
                    stage_h2t(b - 1, 1)

            modulation(0, 2)
            act.wait_ge(col_ready, 1)
            normalise(0)
            modulation(2, 2 * B)
            for half in range(2):
                transposed(0, 0, half)
            act.wait_ge(small_loaded, 48)
            for half in range(2):
                queries(0, 0, half)
            batches(act, batch)

            def relu(n, w, par):
                for c in range(C):
                    act.wait_ge(up_ready, C * n + c + 1)
                    nc.scalar.activation(hidden[par][:, c, :], score[:, c, :], ACT.Relu,
                                         bias=w[:, B1_AT + c:B1_AT + c + 1]).then_inc(hidden_ready, 1)

            keep_h2t(B - 2)
            gap_exponent(B - 2)
            act.wait_ge(value_step, G * B)
            act.wait_ge(shared_loaded, 16)
            relu(0, w_shared, 0)
            second_copy(B - 2)
            relu(1, w_shared, 1)
            stage_h2t(B - 1, 0)
            relu(2, w_shared, 0)
            stage_h2t(B - 1, 1)
            keep_h2t(B - 1)
            relu(3, w_shared, 1)
            gap_exponent(B - 1)
            for n in range(4, FRONT - 1):
                relu(n, w_shared, n % 2)
            second_copy(B - 1)
            relu(FRONT - 1, w_shared, 1)

            def expert(j, par):
                act.wait_ge(xt_ps_ready, j + 1)
                act.wait_ge(up_ready, C * (FRONT + j))
                nc.scalar.activation(tile_xt, xt_ps, ACT.Copy).then_inc(xt_ready, 1)
                relu(FRONT + j, w_exp[par], par)

            with act.Fori(0, ROW_TILES // RING) as i:
                for par in range(RING):
                    expert(RING * i + par, par)
            with act.Fori(FRONT // 2, B) as b:
                for half in range(2):
                    relu(ROW_TILES + 2 * b + half, w_shared, half)

        @block.vector
        def _(dve):
            lw_chain = Chain(dve, lw_step, 0)
            dve.wait_ge(distance_ready, 1)
            lw_chain(nc.vector.scalar_tensor_tensor(out=lw[:, :], in0=lw_mask[:, :], scalar=-1.0, in1=lw_mask[:, :], op0=ALU.mult, op1=ALU.max))
            step = Chain(dve, silu_step, 0)
            dve.wait_ge(silu_exp, 1)
            step(nc.vector.tensor_scalar(silu[:, :], silu[:, :], 1.0, None, ALU.add))
            step(nc.vector.reciprocal(silu[:, :], silu[:, :]))
            step(nc.vector.tensor_tensor(silu[:, :], silu[:, :], c_sb[:, :], ALU.mult))
            nc.vector.tensor_copy(silu_b[:, :, :], silu[:, :].rearrange("p (b o) -> p b o", o=1).to_broadcast([P, B, P])).then_inc(silu_ready, 1)

            def moments_of(b, st, mom, chain, done, rows):
                step = Chain(dve, chain, b)
                wait_alone(dve, rows, (done, b))
                for g in range(G):
                    ins = nc.vector.bn_stats(st[:, g, :], res[:, bass.ds(b * G + g, 1), :].rearrange("p o d -> p (o d)"))
                step(ins, wait=False)
                wait_alone(dve, (step.sem, step.now()))
                for g in range(G):
                    ins = nc.vector.bn_aggr(mom[:, g, :], st[:, g, :])
                ins.then_inc(done, 1)

            def moments_1(b):
                moments_of(b, stats, moments[:, b * G:(b + 1) * G, :], ln1_step, ln1_moments,
                           (x_in[min(b, 2)], 16 * (1 if b < 2 else B - 2)))

            def shift_1(b0, b1):
                dve.wait_ge(ln1_rstd, b1)
                nc.vector.scalar_tensor_tensor(out=shift[:, b0 * G:b1 * G], in0=moments[:, b0 * G:b1 * G, 0], scalar=-1.0,
                                               in1=rstd[:, b0 * G:b1 * G], op0=ALU.mult, op1=ALU.mult).then_inc(ln1_ready, b1 - b0)

            def moments_2(b):
                moments_of(b, stats2, moments2, ln2_step, ln2_moments, (value_used, b + 1))

            moments_1(0)
            dve.wait_ge(col_ps_ready, 1)
            nc.vector.tensor_copy(mod_col[:, 0:2, :].rearrange("p m b -> p (m b)"), misc[:, 0:2 * B])
            nc.vector.tensor_scalar(mod_col[:, 2:4, :].rearrange("p m b -> p (m b)"), misc[:, 2 * B:4 * B], 1.0, None, ALU.add).then_inc(col_ready, 1)
            shift_1(0, 1)
            lw_chain(nc.vector.tensor_scalar(lw[:, :], lw[:, :], EPS_ATT, None, ALU.add))
            lw_chain(nc.vector.reciprocal(lw[:, :], lw[:, :]))
            lw_chain(nc.vector.scalar_tensor_tensor(out=lw[:, :], in0=lw_mask[:, :], scalar=0.0, in1=lw[:, :], op0=ALU.not_equal, op1=ALU.mult))
            moments_1(1)
            dve.wait_ge(const_ready, 1)
            nc.vector.memset(den[:, :], 0.0)
            shift_1(1, 2)

            def normalise_2(b):
                dve.wait_ge(ln2_rstd, b + 1)
                wait(dve, ln2_h, b)
                for g in range(G):
                    ins = nc.vector.tensor_scalar(xhat2[:, g, :], res[:, bass.ds(b * G + g, 1), :].rearrange("p o d -> p (o d)"),
                                                  moments2[:, g, 0:1], rstd2[:, g:g + 1], ALU.subtract, ALU.mult)
                ins.then_inc(ln2_xhat, 1)

            def weigh(b, t):
                dve.wait_ge(score_ready, G * b + t + 1)
                wait(dve, value_step, G * b + t - 3)
                at = (G - 1 - t) * P
                nc.vector.tensor_tensor(prob[:, t % 4, :].rearrange("p (h n) -> p h n", h=2), score[:, 2 * (t % 2):2 * (t % 2) + 2, :],
                                        lw[:, at:at + S].rearrange("p (h n) -> p h n", h=2), ALU.mult).then_inc(score_used, 1)

            def clear_diagonal(b, t):
                dve.wait_ge(exp_done, G * b + t + 1)
                own = prob[:, t % 4, t * P:(t + 1) * P]
                nc.vector.tensor_tensor(own, own, offdiag[:, :], ALU.mult).then_inc(prob_ready, 1)

            def attend(b):
                dve.wait_ge(value_step, G * b + G)
                step = Chain(dve, att_step, b)
                for i in range(3):
                    n = min(3, G - 3 * i)
                    col = value[:, i, 0:n * (D + 1)].rearrange("p (s d) -> p s d", d=D + 1)[:, :, D]
                    ins = nc.vector.tensor_scalar(den[:, 3 * i:3 * i + n], col, EPS_ATT, None, ALU.add)
                step(ins)
                nc.vector.reciprocal(rden[:, :], den[:, :]).then_inc(rden_ready, 1)
                dve.wait_ge(rden_ready, b + 1)
                for s in range(G):
                    r = res[:, bass.ds(b * G + s, 1), :].rearrange("p o d -> p (o d)")
                    ins = nc.vector.scalar_tensor_tensor(out=r, in0=value_at(s), scalar=rden[:, s:s + 1], in1=r, op0=ALU.mult, op1=ALU.add)
                ins.then_inc(value_used, 1)

            def choose(b):
                dve.wait_ge(logits_ps_ready, b + 1)
                step = Chain(dve, route_step, ROUTE * b)
                nc.vector.tensor_copy(logits[:, :, :].rearrange("p g e -> p (g e)"), misc[:, 0:G * E]).then_inc(logits_ready, 1)
                wait_alone(dve, (logits_ready, b + 1))
                for g in range(G):
                    ins = nc.vector.max(top_v[:, g, :], logits[:, g, :])
                step(ins, wait=False)
                wait_alone(dve, (step.sem, step.now()))
                for g in range(G):
                    ins = nc.vector.max_index(top_i[:, g, :], top_v[:, g, :], logits[:, g, :])
                step(ins, wait=False)
                nc.vector.tensor_tensor(gap[:, :], top_v[:, :, 1], top_v[:, :, 0], ALU.subtract).then_inc(gap_ready, 1)
                dve.wait_ge(route_step, ROUTE * b + step.n)
                step(nc.vector.tensor_copy(top_f[:, :, :], top_i[:, :, :]))
                step(nc.vector.tensor_tensor(hot_1[:, :, :], expert_no[:, :, :], top_f[:, :, 0:1].to_broadcast([P, G, E]), ALU.is_equal), wait=False)
                step(nc.vector.tensor_tensor(hot_2[:, :, :], expert_no[:, :, :], top_f[:, :, 1:2].to_broadcast([P, G, E]), ALU.is_equal))
                step(nc.vector.tensor_tensor(chosen[:, :, :], hot_1[:, :, :], hot_2[:, :, :], ALU.add))
                wait(dve, rank_ps_ready, b)
                for g in range(G):
                    ins = nc.vector.tensor_tensor(earlier[:, g + 1, :], earlier[:, g, :], chosen[:, g, :], ALU.add)
                    if g < G - 1:
                        step(ins)
                ins.then_inc(chosen_ready, 1)
                assert step.n == CHOOSE, step.n

            def assign(b):
                step = Chain(dve, route_step, ROUTE * b + CHOOSE)
                dve.wait_ge(rank_ps_ready, b + 1)
                rank = misc[:, 0:E].rearrange("p (o e) -> p o e", o=1).to_broadcast([P, G, E])
                nc.vector.tensor_tensor(place[:, :, :], earlier[:, 0:G, :], rank, ALU.add).then_inc(rank_used, 1)
                step(nc.vector.tensor_tensor(carry[:, :], carry[:, :], earlier[:, G, :], ALU.add), wait=False)
                dve.wait_ge(rank_used, b + 1)
                step(nc.vector.tensor_tensor(hot_1[:, :, :], hot_1[:, :, :], place[:, :, :], ALU.mult), wait=False)
                step(nc.vector.tensor_tensor(hot_2[:, :, :], hot_2[:, :, :], place[:, :, :], ALU.mult))
                step(nc.vector.tensor_reduce(slot_f[:, 0, :], hot_1[:, :, :], AX.X, ALU.add), wait=False)
                step(nc.vector.tensor_reduce(slot_f[:, 1, :], hot_2[:, :, :], AX.X, ALU.add))
                dve.wait_ge(gap_exp, b + 1)
                step(nc.vector.tensor_scalar(gap_1[:, :], gap_e[:, :], 1.0, None, ALU.add))
                step(nc.vector.reciprocal(w_first[:, :], gap_1[:, :]))
                step(nc.vector.tensor_tensor(w_second[:, :], w_first[:, :], gap_e[:, :], ALU.mult))
                dve.wait_ge(ln2_h, b + 1)
                step(nc.vector.tensor_copy(slot[:, :, :], slot_f[:, :, :]), wait=False)
                step(nc.vector.tensor_copy(row_1[:, :, D + 1], w_first[:, :]), wait=False)
                step(nc.vector.tensor_copy(row_2[:, :, D + 1], w_second[:, :]), wait=False)
                step(nc.vector.tensor_copy(row_1[:, :, D].bitcast(I32), token_no[:, :]), wait=False)
                step(nc.vector.tensor_scalar(row_2[:, :, D].bitcast(I32), token_no[:, :], float(T), None, ALU.add))
                nc.vector.tensor_scalar(token_no[:, :], token_no[:, :], float(S), None, ALU.add).then_inc(slots_ready, 1)
                dve.wait_ge(slots_ready, b + 1)
                assert CHOOSE + step.n == ROUTE, step.n

            ahead = moments_1

            def batch(b, par):
                weigh(b, 0)
                if exists(b - 1):
                    clear_diagonal(b - 1, G - 1)
                if exists(b - 2):
                    choose(b - 2)
                if isinstance(b, int) and b == 0:
                    ahead(2)
                weigh(b, 1)
                clear_diagonal(b, 0)
                if exists(b - 1):
                    attend(b - 1)
                if isinstance(b, int) and b == 0:
                    ahead(3)
                weigh(b, 2)
                clear_diagonal(b, 1)
                if exists(b - 1):
                    moments_2(b - 1)
                if isinstance(b, int) and b == 0:
                    ahead(4)
                weigh(b, 3)
                clear_diagonal(b, 2)
                if exists(b - 2):
                    assign(b - 2)
                weigh(b, 4)
                clear_diagonal(b, 3)
                if exists(b - 1):
                    normalise_2(b - 1)
                if isinstance(b, int) and b == 0:
                    ahead(5)
                for t in range(5, G):
                    weigh(b, t)
                    clear_diagonal(b, t - 1)
                    if isinstance(b, int) and b == 0 and t < G - 1:
                        ahead(t + 1)
                if isinstance(b, int) and b == 0:
                    shift_1(2, B)

            batches(dve, batch)
            clear_diagonal(B - 1, G - 1)
            choose(B - 2)
            attend(B - 1)
            moments_2(B - 1)
            assign(B - 2)
            normalise_2(B - 1)

            def shared(n):
                par, half = n % 2, n % 2
                dve.wait_ge(down_ready, n + 1)
                step = Chain(dve, y_step, 2 * n)
                bias = w_shared[:, B2_AT:PACK].rearrange("p (o d) -> p o d", o=1).to_broadcast([P, K, D])
                step(nc.vector.tensor_tensor(tile_y[par][:, :, :], yacc[par].rearrange("p (k d) -> p k d", k=K), bias, ALU.add))
                gate = mod[:, n // 2:n // 2 + 1, 5, :].to_broadcast([P, K, D])
                step(nc.vector.tensor_tensor(tile_y[par][:, :, :], tile_y[par][:, :, :], gate, ALU.mult))
                r = res[:, (n // 2) * G + K * half:(n // 2) * G + K * half + K, :]
                nc.vector.tensor_tensor(r, r, tile_y[par][:, :, :], ALU.add).then_inc(y_evac, 1)

            shared(0)
            shared(1)
            choose(B - 1)
            shared(2)
            assign(B - 1)
            shared(3)

            dve.wait_ge(total_ps_ready, 1)
            step = Chain(dve, table_step, 0)
            step(nc.vector.tensor_tensor(count[:, :], misc[:, 0:E], region_at[:, :], ALU.subtract))
            step(nc.vector.tensor_scalar(count_i[:, :], count[:, :], float(TILE - 1), None, ALU.add))
            step(nc.vector.tensor_scalar(tiles_i[:, :], count_i[:, :], TILE.bit_length() - 1, None, ALU.arith_shift_right))
            step(nc.vector.tensor_copy(tiles_f[:, :], tiles_i[:, :]))
            step(nc.vector.tensor_copy(ends[:, 0:1], tiles_f[:, 0:1]))
            for e in range(1, E):
                step(nc.vector.tensor_tensor(ends[:, e:e + 1], ends[:, e - 1:e], tiles_f[:, e:e + 1], ALU.add))
            step(nc.vector.tensor_tensor(starts[:, :], ends[:, :], tiles_f[:, :], ALU.subtract))
            ends_b = ends[:, :].rearrange("p (o e) -> p o e", o=1).to_broadcast([P, ROW_TILES, E])
            tiles_b = tiles_f[:, :].rearrange("p (o e) -> p o e", o=1).to_broadcast([P, ROW_TILES, E])
            step(nc.vector.tensor_tensor(past[:, :, :], tile_no[:, :, :], ends_b, ALU.is_ge))
            step(nc.vector.tensor_reduce(tile_e[:, :], past[:, :, :], AX.X, ALU.add))
            step(nc.vector.tensor_tensor(past[:, :, :], past[:, :, :], tiles_b, ALU.mult))
            step(nc.vector.tensor_reduce(tile_s[:, :], past[:, :, :], AX.X, ALU.add))
            step(nc.vector.tensor_tensor(tile_s[:, :], tile_no[:, :, 0], tile_s[:, :], ALU.subtract))
            step(nc.vector.tensor_scalar(tile_u[:, :], tile_e[:, :], float(E), -float(TILE), ALU.is_lt, ALU.mult))
            step(nc.vector.tensor_tensor(tile_s[:, :], tile_s[:, :], tile_u[:, :], ALU.mult))
            step(nc.vector.scalar_tensor_tensor(out=tile_r[:, :], in0=tile_e[:, :], scalar=float(REGION), in1=tile_s[:, :],
                                                op0=ALU.mult, op1=ALU.subtract))
            step(nc.vector.tensor_copy(table_r[:, :], tile_r[:, :]), wait=False)
            step(nc.vector.tensor_scalar(table_e[:, :], tile_e[:, :], float(E - 1), None, ALU.min))
            nc.vector.tensor_tensor(pad_at[:, :], count[:, :], region_at[:, :], ALU.add).then_inc(table_ready, 1)

            for n in range(4, FRONT):
                shared(n)

            def expert(j, i, par, first=False):
                dve.wait_ge(down_ready, FRONT + j + 1)
                if not first:
                    dve.wait_ge(y_sent[par], 16 * K * i)
                bias = w_exp[par][:, B2_AT:PACK].rearrange("p (o d) -> p o d", o=1).to_broadcast([P, K, D])
                nc.vector.tensor_tensor(tile_y[par][:, :, :], yacc[par].rearrange("p (k d) -> p k d", k=K), bias, ALU.add).then_inc(y_evac, 1)
                dve.wait_ge(y_evac, FRONT + j + 1)
                for k in range(K):
                    ins = nc.vector.tensor_scalar(tile_y[par][:, k, :], tile_y[par][:, k, :], tile_x[par][:, k, D + 1:D + 2], None, ALU.mult)
                ins.then_inc(y_ready, 1)

            for j in range(RING):
                expert(j, 0, j, True)
            with dve.Fori(1, ROW_TILES // RING) as i:
                for par in range(RING):
                    expert(RING * i + par, i, par)

            for par in range(2):
                dve.wait_ge(y_sent[par], 16 * K * (ROW_TILES // RING))
            with dve.Fori(FRONT // 2, B) as b:
                for half in range(2):
                    n = ROW_TILES + 2 * b + half
                    dve.wait_ge(down_ready, n + 1)
                    y = tile_y[half][:, :, :]
                    bias = w_shared[:, B2_AT:PACK].rearrange("p (o d) -> p o d", o=1).to_broadcast([P, K, D])
                    nc.vector.tensor_tensor(y, yacc[half].rearrange("p (k d) -> p k d", k=K), bias, ALU.add).then_inc(y_evac, 1)
                    dve.wait_ge(y_evac, n + 1)
                    dve.wait_ge(z_loaded[half], 32 * (b - FRONT // 2 + 1))
                    step = Chain(dve, fin_step, 3 * (2 * b + half - FRONT))
                    for k in range(2):
                        step(nc.vector.tensor_tensor(y, y, z_half[half][k].rearrange("p (k d) -> p k d", k=K), ALU.add))
                    gate = mod[:, bass.ds(b, 1), 5, :].to_broadcast([P, K, D])
                    step(nc.vector.tensor_tensor(y, y, gate, ALU.mult))
                    r = res[:, bass.ds(b * G + K * half, K), :]
                    nc.vector.tensor_tensor(r, r, y, ALU.add).then_inc(fin_ready, 1)

        @block.tensor
        def _(pe):
            pe.wait_ge(cond_loaded, 32)
            pe.wait_ge(silu_ready, 1)
            for i, m in enumerate((0, 3, 1, 4)):
                ins = nc.tensor.matmul(misc[:, i * B:(i + 1) * B], wmod_sb[:, m * D:(m + 1) * D], silu[:, :], start=True, stop=True)
            ins.then_inc(col_ps_ready, 1)
            for n in range(2 * B):
                if n >= 4:
                    pe.wait_ge(mod_evac, n - 3)
                half = (n % 2) * (MOD // 2)
                nc.tensor.matmul(score[:, n % 4, 0:MOD // 2], silu_b[:, n // 2, :], wmod_sb[:, half:half + MOD // 2],
                                 start=True, stop=True).then_inc(mod_ps_ready, 1)
            pe.wait_ge(const_ready, 1)
            pe.wait_ge(col_ready, 1)

            def misc_rows(src, half):
                for k in range(4):
                    ins = nc.tensor.transpose(misc[:, k * P:(k + 1) * P], src[:, 4 * half + k, :], ident[:, :])
                return ins

            def transpose_h(b, half):
                pe.wait_ge(ln1_xhat, b + 1)
                if half:
                    pe.wait_ge(ht_ready, 2 * b + 1)
                elif exists(b - 3):
                    pe.wait_ge(rank_used, b - 2)
                misc_rows(xhat, half).then_inc(ht_ps_ready, 1)

            def queries(b, par, half):
                pe.wait_ge(ht_ready, 2 * b + 2)
                if half:
                    pe.wait_ge(qt_ready, 2 * b + 1)
                nc.tensor.matmul(misc[:, :], watt_sb[:, :], h_t[par][:, half * 512:half * 512 + 512],
                                 start=True, stop=True).then_inc(qt_ps_ready, 1)

            def scores(b, par, t):
                if t == 0:
                    pe.wait_ge(qt_ready, 2 * b + 2)
                wait(pe, score_used, G * b + t - 1)
                for half in range(2):
                    ins = nc.tensor.matmul(score[:, 2 * (t % 2) + half, :], h_t[par][:, t * P:(t + 1) * P],
                                           q_t[par][:, half * 512:half * 512 + 512], start=True, stop=True)
                ins.then_inc(score_ready, 1)

            def values(b, par, t):
                pe.wait_ge(prob_ready, G * b + t + 1)
                if t == 0:
                    pe.wait_ge(gated, b + 1)
                    wait(pe, value_used, b)
                for s in range(G):
                    c0 = (s % 3) * (D + 1)
                    ins = nc.tensor.matmul(value[:, s // 3, c0:c0 + D + 1], prob[:, t % 4, s * P:(s + 1) * P], h_ones[:, par, t, :],
                                           start=(t == 0 and s % 3 == 0), stop=(t == G - 1), skip_group_check=True)
                ins.then_inc(value_step, 1)

            def transpose_h2(b, half):
                pe.wait_ge(ln2_xhat, b + 1)
                if half:
                    pe.wait_ge(h2t_staged, 2 * b + 1)
                misc_rows(xhat2, half).then_inc(h2t_ps_ready, 1)

            def gate_logits(b):
                pe.wait_ge(h2t_staged, 2 * b + 2)
                for g in range(G):
                    ins = nc.tensor.matmul(misc[:, g * E:(g + 1) * E], h2_ts[:, g * P:(g + 1) * P], wg_sb[:, :], start=True, stop=True)
                ins.then_inc(logits_ps_ready, 1)

            def ranks(b):
                pe.wait_ge(chosen_ready, b + 1)
                nc.tensor.matmul(misc[:, 0:E], before[:, :], earlier[:, G, :], start=True, stop=False)
                nc.tensor.matmul(misc[:, 0:E], ones[:, :], carry[:, :], start=False, stop=True).then_inc(rank_ps_ready, 1)

            def batch(b, par):
                scores(b, par, 0)
                if exists(b - 1):
                    values(b - 1, 1 - par, G - 2)
                if exists(b - 2):
                    gate_logits(b - 2)
                scores(b, par, 1)
                if exists(b - 1):
                    values(b - 1, 1 - par, G - 1)
                scores(b, par, 2)
                if exists(b - 2):
                    ranks(b - 2)
                scores(b, par, 3)
                values(b, par, 0)
                if exists(b + 1):
                    transpose_h(b + 1, 0)
                scores(b, par, 4)
                values(b, par, 1)
                if exists(b + 1):
                    transpose_h(b + 1, 1)
                scores(b, par, 5)
                values(b, par, 2)
                if exists(b + 1):
                    queries(b + 1, 1 - par, 0)
                scores(b, par, 6)
                values(b, par, 3)
                if exists(b + 1):
                    queries(b + 1, 1 - par, 1)
                values(b, par, 4)
                if exists(b - 1):
                    if exists(b + 1):
                        pe.wait_ge(qt_ready, 2 * b + 4)
                    else:
                        pe.wait_ge(rank_used, b - 1)
                    transpose_h2(b - 1, 0)
                scores(b, par, 7)
                values(b, par, 5)
                if exists(b - 1):
                    transpose_h2(b - 1, 1)

            transpose_h(0, 0)
            transpose_h(0, 1)
            pe.wait_ge(small_loaded, 48)
            queries(0, 0, 0)
            queries(0, 0, 1)
            batches(pe, batch)
            values(B - 1, 1, G - 2)
            gate_logits(B - 2)
            values(B - 1, 1, G - 1)

            def up(n, w, src, first=False):
                for c in range(C):
                    if not first:
                        pe.wait_ge(hidden_ready, C * (n - 1) + c + 1)
                    nc.tensor.matmul(score[:, c, :], w[:, c * P:(c + 1) * P], src, start=True, stop=True).then_inc(up_ready, 1)

            def down(n, w, par, first=False):
                if not first:
                    pe.wait_ge(y_evac, n - 1)
                for c in range(C):
                    pe.wait_ge(hidden_ready, C * n + c + 1)
                    for k in range(K):
                        ins = nc.tensor.matmul(yacc[par][:, k * D:(k + 1) * D], hidden[par][:, c, k * P:(k + 1) * P],
                                               w[:, W2_AT + c * D:W2_AT + (c + 1) * D],
                                               start=(c == 0 and k == 0), stop=(c == C - 1), skip_group_check=True)
                ins.then_inc(down_ready, 1)

            pe.wait_ge(h2t_kept, FRONT // 2)
            pe.wait_ge(shared_loaded, 16)
            pe.wait_ge(score_used, G * B)
            pe.wait_ge(value_used, B)

            def shared_up(n):
                up(n, w_shared, h2_t[:, n * TILE:(n + 1) * TILE], first=(n == 0))

            def shared_down(n):
                down(n, w_shared, n % 2, first=(n < 2))

            shared_up(0)
            shared_down(0)
            ranks(B - 2)
            shared_up(1)
            shared_down(1)
            pe.wait_ge(rank_used, B - 1)
            transpose_h2(B - 1, 0)
            shared_up(2)
            transpose_h2(B - 1, 1)
            shared_down(2)
            gate_logits(B - 1)
            shared_up(3)
            shared_down(3)
            ranks(B - 1)
            shared_up(4)
            pe.wait_ge(slots_ready, B)
            nc.tensor.matmul(misc[:, 0:E], ones[:, :], carry[:, :], start=True, stop=True).then_inc(total_ps_ready, 1)
            shared_down(4)
            for n in range(5, FRONT):
                shared_up(n)
                shared_down(n)
            pe.wait_ge(table_ready, 1)

            def transpose_rows(j, i, par, first=False):
                pe.wait_ge(x_loaded[par], 16 * (i + 1))
                if not first:
                    pe.wait_ge(xt_ready, j)
                for k in range(K):
                    ins = nc.tensor.transpose(xt_ps[:, k * P:(k + 1) * P], tile_x[par][:, k, 0:D], ident[:, :])
                ins.then_inc(xt_ps_ready, 1)

            def expert_up(j, i, par):
                pe.wait_ge(xt_ready, j + 1)
                pe.wait_ge(w_loaded[par], 16 * (i + 1))
                up(FRONT + j, w_exp[par], tile_xt)

            transpose_rows(0, 0, 0, True)

            def expert(i, par, last=False):
                j = RING * i + par
                expert_up(j, i, par)
                if not last:
                    transpose_rows(j + 1, i + (par + 1) // RING, (par + 1) % RING)
                down(FRONT + j, w_exp[par], par)

            with pe.Fori(0, ROW_TILES // RING - 1) as i:
                for par in range(RING):
                    expert(i, par)
            for par in range(RING):
                expert(ROW_TILES // RING - 1, par, last=(par == RING - 1))

            pe.wait_ge(h2t_kept, B)
            with pe.Fori(FRONT // 2, B) as b:
                for half in range(2):
                    n = ROW_TILES + 2 * b + half
                    up(n, w_shared, h2_t[:, bass.ds((2 * b + half) * TILE, TILE)])
                    down(n, w_shared, half)


def kernel(**inputs):
    from concourse import bacc
    from concourse.bass_utils import run_bass_kernel_spmd

    a = {k.removeprefix("L0_"): np.asarray(v) for k, v in inputs.items()}

    def chunks(w):
        return w.reshape(C, P, D).transpose(1, 0, 2).reshape(P, C * D)

    def pack(w1, b1, w2, b2):
        return np.concatenate([w1, chunks(w2), b1.reshape(C, P).T, np.broadcast_to(b2, (P, D))], axis=1)

    packs = [pack(a["ffn_W1"][e], a["ffn_b1"][e], a["ffn_W2"][e], a["ffn_b2"][e]) for e in range(E)]
    packs.append(pack(a["ffn_Ws1"], a["ffn_bs1"], a["ffn_Ws2"], a["ffn_bs2"]))
    arrays = {
        "x": a["attn_x"].reshape(T, D), "c_t": a["c"].T, "wmod": a["wmod"], "w_att": a["attn_W"],
        "b_att": a["attn_b"].reshape(D, 1), "wg": a["ffn_Wg"], "packs": np.stack(packs),
    }
    arrays = {k: np.ascontiguousarray(v) for k, v in arrays.items()}
    nc = bacc.Bacc("TRN2", target_bir_lowering=False, num_devices=1)
    args = [nc.dram_tensor(k, v.shape, mybir.dt.from_np(v.dtype), kind="ExternalInput").ap() for k, v in arrays.items()]
    args.append(nc.dram_tensor("out", (T, D), F32, kind="ExternalOutput").ap())
    adaln_moe(nc, *args)
    r = run_bass_kernel_spmd(nc, [arrays], core_ids=[0])
    return r.results[0]["out"].reshape(B, S, D)
```

```python
from contextlib import ExitStack

import numpy as np

import concourse.bass as bass
from concourse import mybir

F32 = mybir.dt.float32
F32R = mybir.dt.float32r
I32 = mybir.dt.int32
U32 = mybir.dt.uint32
ALU = mybir.AluOpType
ACT = mybir.ActivationFunctionType
AX = mybir.AxisListType

P = 128
B, S, D = 8, 1024, 128
G = S // P
T = B * S
E, F = 8, 512
C = F // P
TILE = 512
SMALL = 256
K = TILE // P
REGION = T + SMALL
ROW = D + 2
LARGE_TILES = 24
SMALL_TILES = (2 * T - LARGE_TILES * TILE) // SMALL + E - 1
ROW_TILES = LARGE_TILES + SMALL_TILES
SPARE = E * REGION
X_ROWS = SPARE + SMALL
Z_ROWS = 2 * T
NOWHERE = 2 * Z_ROWS
W2_AT, B1_AT, B2_AT = F, F + C * D, F + C * D + C
PACK = B2_AT + D
MOD = 6 * D
EPS_ATT = 1e-7
EPS_LN = 1e-5
SHARED_TILES = T // TILE
FRONT = 8
RING = 3
CYCLE = 2 * RING
CYCLES = (ROW_TILES + 1) // CYCLE
AHEAD = 2 + (B - 2) // 2
assert LARGE_TILES * TILE <= 2 * T - E * (TILE - 1) + TILE - 1
assert LARGE_TILES == SMALL_TILES + 1 and ROW_TILES + 1 == CYCLES * CYCLE


def rows_of(pos):
    return TILE if pos % 2 == 0 else SMALL


def sent_before(i, pos):
    n = 16 * (TILE + SMALL) // P * i
    return n if pos < RING else n + 16 * rows_of(pos - RING) // P


def sent_in_all(par):
    return sent_before(CYCLES, par) - (16 * rows_of(CYCLE - 1) // P if par == RING - 1 else 0)


def following(i, pos):
    return (i, pos + 1) if pos + 1 < CYCLE else (i + 1, 0)


def loads(i, pos):
    return 16 * (2 * i + pos // RING + 1)


class Chain:

    def __init__(self, eng, sem, start):
        self.eng, self.sem, self.start, self.n = eng, sem, start, 0

    def __call__(self, ins, wait=True):
        ins.then_inc(self.sem, 1)
        self.n += 1
        if wait:
            self.eng.wait_ge(self.sem, self.now())

    def now(self):
        return self.start + self.n


def adaln_moe(nc, x, c_t, wmod, w_att, b_att, wg, packs, out):
    with ExitStack() as ctx:
        def sb(name, shape, dt=F32):
            return ctx.enter_context(nc.sbuf_tensor(name, shape, dt))

        def ps(name, shape):
            return ctx.enter_context(nc.psum_tensor(name, shape, F32))

        def sem(name):
            return ctx.enter_context(nc.semaphore(name))

        rows_x = nc.dram_tensor("rows_x", [X_ROWS, ROW], F32).ap()
        rows_z = nc.dram_tensor("rows_z", [Z_ROWS, D], F32).ap()

        ident = sb("ident", [P, P])
        offdiag = sb("offdiag", [P, P])
        before = sb("before", [P, P])
        ones = sb("ones", [P, P])
        lw = sb("lw", [P, (2 * G - 1) * P])
        minus_half = sb("minus_half", [P, B * G])
        expert_no = sb("expert_no", [P, G, E])
        token_no = sb("token_no", [P, G])
        region_at = sb("region_at", [P, E])
        tile_no = sb("tile_no", [P, LARGE_TILES, E])
        pad_rows = sb("pad_rows", [P, SMALL // P, ROW])
        c_sb = sb("c_sb", [P, B])
        silu = sb("silu", [P, B])
        watt_sb = sb("watt_sb", [D, D])
        batt_sb = sb("batt_sb", [D, 1])
        wg_sb = sb("wg_sb", [D, E])
        w_shared = sb("w_shared", [P, PACK])
        w_ring = sb("w_ring", [P, RING * PACK])
        w_exp = [w_ring[:, i * PACK:(i + 1) * PACK] for i in range(RING)]
        wmod_sb = w_exp[0][:, 0:MOD]
        mod = sb("mod", [P, B, 5, D])
        mod_col = sb("mod_col", [D, 4, B])
        res = sb("res", [P, B * G, D])
        h2_t = sb("h2_t", [D, T])
        lw_mask = h2_t[:, 0:(2 * G - 1) * P]
        stats = sb("stats", [P, G, 6])
        moments = sb("moments", [P, B * G, 2])
        rstd = sb("rstd", [P, B * G])
        shift = sb("shift", [P, B * G])
        stats2 = sb("stats2", [P, G, 6])
        moments2 = sb("moments2", [P, G, 2])
        rstd2 = sb("rstd2", [P, G])
        xhat = sb("xhat", [P, G, D])
        xhat2 = sb("xhat2", [P, G, D])
        half_sign = xhat2
        h_ones = w_ring[:, PACK:PACK + 2 * G * (D + 1)].rearrange("p (o g d) -> p o g d", o=2, g=G)
        work = sb("work", [P, 4 * S + 2 * G * ROW])
        prob = work[:, 0:4 * S].rearrange("p (t s) -> p t s", t=4)
        att_gate = work[:, 4 * S:5 * S].rearrange("p (b d) -> p b d", b=B)
        silu_b = work[:, 5 * S:6 * S].rearrange("p (b q) -> p b q", b=B)
        h_hi, h_lo, q_hi, q_lo = ([sb(f"{n}{i}", [D, S], F32R) for i in range(2)] for n in ("h_hi", "h_lo", "q_hi", "q_lo"))
        watt_hi = sb("watt_hi", [D, D], F32R)
        watt_lo = sb("watt_lo", [D, D], F32R)
        den = sb("den", [P, G])
        rden = sb("rden", [P, G])
        row_1 = sb("row_1", [P, G, ROW])
        row_2 = sb("row_2", [P, G, ROW])
        last_1 = work[:, 4 * S:4 * S + G * ROW].rearrange("p (g r) -> p g r", g=G)
        last_2 = work[:, 4 * S + G * ROW:4 * S + 2 * G * ROW].rearrange("p (g r) -> p g r", g=G)
        h2_ts = sb("h2_ts", [D, S])
        logits = sb("logits", [P, G, E])
        top_v = sb("top_v", [P, G, E])
        top_i = sb("top_i", [P, G, E], U32)
        top_f = sb("top_f", [P, G, E])
        hot_1 = sb("hot_1", [P, G, E])
        hot_2 = sb("hot_2", [P, G, E])
        chosen = sb("chosen", [P, G, E])
        earlier = sb("earlier", [P, G + 1, E])
        carry = sb("carry", [P, E])
        place = sb("place", [P, G, E])
        slot_f = sb("slot_f", [P, 2, G])
        slot = sb("slot", [P, 2, G], I32)
        last_slot = sb("last_slot", [P, 2, G], I32)
        gap = sb("gap", [P, G])
        gap_e = sb("gap_e", [P, G])
        gap_1 = sb("gap_1", [P, G])
        w_first = sb("w_first", [P, G])
        w_second = sb("w_second", [P, G])
        count = sb("count", [P, E])
        rest = sb("rest", [P, E])
        count_i = sb("count_i", [P, E], I32)
        tiles_i = sb("tiles_i", [P, E], I32)
        sums = sb("sums", [P, 2, 4, E // 2 + E])
        row_at = sb("row_at", [P, E + 1])
        row_step = sb("row_step", [P, E])
        past = sb("past", [P, LARGE_TILES, E])
        tile_e = sb("tile_e", [P, LARGE_TILES])
        tile_r = sb("tile_r", [P, LARGE_TILES])
        table_e = sb("table_e", [P, LARGE_TILES, 2], I32)
        table_r = sb("table_r", [P, LARGE_TILES, 2], I32)
        pad_at = sb("pad_at", [P, E], I32)
        tile_x = [lw[:, i * K * ROW:(i + 1) * K * ROW].rearrange("p (k r) -> p k r", k=K) for i in range(RING)]
        tags = [sb(f"tags{i}", [P, K, 2]) for i in range(RING)]
        xt_hi, xt_lo = ([h_hi[par][:, i * TILE:(i + 1) * TILE] for par in range(2)] for i in range(2))
        w1_hi, w1_lo = ([h_lo[par][:, i * F:(i + 1) * F] for par in range(2)] for i in range(2))
        hidden = [work[:, i * C * TILE:(i + 1) * C * TILE].rearrange("p (c n) -> p c n", c=C) for i in range(RING)]
        tile_y = [sb(f"tile_y{i}", [P, K, D]) for i in range(RING)]
        h_f = [tile_y[i][:, :, :].rearrange("p k d -> p (k d)") for i in range(2)]

        score = ps("score", [P, 4, 512])
        value = ps("value", [P, 3, 512])
        misc = ps("misc", [P, 512])
        yacc = [value[:, 0, :], value[:, 1, :], misc[:, :]]
        xt_ps = value[:, 2, :]

        def value_at(s):
            return value[:, s // 3, (s % 3) * (D + 1):(s % 3) * (D + 1) + D]

        cond_loaded = sem("cond_loaded")
        small_loaded = sem("small_loaded")
        x_in = [sem(f"x_in{i}") for i in range(3)]
        shared_loaded = sem("shared_loaded")
        const_ready = sem("const_ready")
        const_step = sem("const_step")
        places_passed = sem("places_passed")
        distance_ready = sem("distance_ready")
        distance_abs = sem("distance_abs")
        silu_step = sem("silu_step")
        lw_step = sem("lw_step")
        last_step = sem("last_step")
        silu_exp = sem("silu_exp")
        silu_ready = sem("silu_ready")
        col_ps_ready = sem("col_ps_ready")
        col_ready = sem("col_ready")
        mod_ps_ready = sem("mod_ps_ready")
        mod_evac = sem("mod_evac")
        mod_step = sem("mod_step")

        ln1_step = sem("ln1_step")
        ln1_moments = sem("ln1_moments")
        ln1_pool_step = sem("ln1_pool_step")
        ln1_rstd = sem("ln1_rstd")
        ln1_ready = sem("ln1_ready")
        ln1_xhat = sem("ln1_xhat")
        gate_step = sem("gate_step")
        gated = sem("gated")
        ht_ps_ready = sem("ht_ps_ready")
        ht_ready = sem("ht_ready")
        h_hi_ready = sem("h_hi_ready")
        h_split = sem("h_split")
        q_hi_ready = sem("q_hi_ready")
        watt_hi_ready = sem("watt_hi_ready")
        watt_split = sem("watt_split")
        qt_ps_ready = sem("qt_ps_ready")
        qt_ready = sem("qt_ready")
        score_ready = sem("score_ready")
        score_used = sem("score_used")
        tanh_done = sem("tanh_done")
        exp_done = sem("exp_done")
        prob_ready = sem("prob_ready")
        value_step = sem("value_step")
        value_used = sem("value_used")
        att_step = sem("att_step")
        rden_ready = sem("rden_ready")
        ln2_step = sem("ln2_step")
        ln2_moments = sem("ln2_moments")
        ln2_pool_step = sem("ln2_pool_step")
        ln2_rstd = sem("ln2_rstd")
        ln2_xhat = sem("ln2_xhat")
        ln2_mod_step = sem("ln2_mod_step")
        ln2_h = sem("ln2_h")
        second_rows = sem("second_rows")
        last_second = sem("last_second")
        h2t_ps_ready = sem("h2t_ps_ready")
        h2t_staged = sem("h2t_staged")
        h2t_kept = sem("h2t_kept")
        logits_ps_ready = sem("logits_ps_ready")
        logits_ready = sem("logits_ready")
        route_step = sem("route_step")
        chosen_ready = sem("chosen_ready")
        gap_ready = sem("gap_ready")
        gap_exp = sem("gap_exp")
        rank_ps_ready = sem("rank_ps_ready")
        rank_used = sem("rank_used")
        carried = sem("carried")
        slots_ready = sem("slots_ready")
        scattered = sem("scattered")

        total_ps_ready = sem("total_ps_ready")
        table_step = sem("table_step")
        counted = sem("counted")
        table_ready = sem("table_ready")
        padded = sem("padded")
        x_loaded = [sem(f"x_loaded{i}") for i in range(RING)]
        w_loaded = [sem(f"w_loaded{i}") for i in range(RING)]
        xt_ps_ready = sem("xt_ps_ready")
        x_hi_ready = sem("x_hi_ready")
        x_split = sem("x_split")
        w_hi_ready = sem("w_hi_ready")
        w_split = sem("w_split")
        tagged = sem("tagged")
        up_ready = sem("up_ready")
        hidden_ready = sem("hidden_ready")
        down_ready = sem("down_ready")
        y_evac = sem("y_evac")
        y_step = sem("y_step")
        y_ready = sem("y_ready")
        y_sent = [sem(f"y_sent{i}") for i in range(RING)]
        z_loaded = [sem(f"z_loaded{i}") for i in range(2)]
        fin_step = sem("fin_step")
        results_added = sem("results_added")
        bias_step = sem("bias_step")
        fin_ready = sem("fin_ready")
        front_loaded = [sem(f"front_loaded{i}") for i in range(2)]
        front_step = sem("front_step")
        front_stored = sem("front_stored")
        stored = sem("stored")

        x_v = x.rearrange("(b p g) d -> p b (g d)", b=B, p=P, g=G)
        out_v = out.rearrange("(b p g) d -> b p (g d)", b=B, p=P, g=G)
        z_v = rows_z.rearrange("(k b p g) d -> k b p (g d)", k=2, b=B, p=P, g=G)
        ROUTE, CHOOSE = 25, 13

        z_half = [[hidden[2][:, 2 * i + k, :] for k in range(2)] for i in range(2)]
        z_front = [[xhat[:, :, :].rearrange("p g d -> p (g d)"), xhat2[:, :, :].rearrange("p g d -> p (g d)")],
                   [r[:, :, :].rearrange("p g r -> p (g r)")[:, 0:G * D] for r in (row_1, row_2)]]

        block = ctx.enter_context(nc.Block())

        def wait(eng, on, count):
            if not isinstance(count, int) or count > 0:
                eng.wait_ge(on, count)

        def exists(b):
            return not isinstance(b, int) or 0 <= b < B

        def batches(eng, batch):
            batch(0, 0)
            batch(1, 1)
            with eng.Fori(1, B // 2 - 1) as i:
                for par in range(2):
                    batch(2 * i + par, par)
            batch(B - 2, 0)
            batch(B - 1, 1)

        def wait_alone(eng, *waits):
            for on, v in waits:
                if not isinstance(v, int) or v > 0:
                    eng.wait_ge(on, v)
                    eng.sem_inc(places_passed, 1)

        @block.sync
        def _(sp):
            for b in range(B):
                sp.dma_start(res[:, b * G:(b + 1) * G, :].rearrange("p g d -> p (g d)"), x_v[:, b, :]).then_inc(x_in[min(b, 2)], 16)
            sp.dma_start(w_shared[:, :], packs[E]).then_inc(shared_loaded, 16)

            def load_weights(j, par):
                e = sp.value_load(table_e[0:1, :, :].rearrange("p m o -> p (m o)")[:, bass.ds(j, 1)], min_val=0, max_val=E - 1)
                sp.dma_start(w_exp[par][:, :], packs[bass.ds(e, 1), :, :].rearrange("e p n -> (e p) n")).then_inc(w_loaded[par], 16)

            def load_rows(j, pos):
                par, n = pos % RING, rows_of(pos)
                r = sp.value_load(table_r[0:1, :, :].rearrange("p m o -> p (m o)")[:, bass.ds(j, 1)], min_val=0, max_val=X_ROWS - n)
                sp.dma_start(tile_x[par][:, 0:n // P, :].rearrange("p k r -> p (k r)"),
                             rows_x[bass.ds(r, n), :].rearrange("(p k) r -> p (k r)", p=P)).then_inc(x_loaded[par], 16)

            sp.wait_ge(const_ready, 1)
            sp.dma_start(rows_x[SPARE:X_ROWS, :].rearrange("(p k) r -> p (k r)", p=P),
                         pad_rows[:, :, :].rearrange("p k r -> p (k r)")).then_inc(padded, 16)
            sp.wait_ge(counted, 1)
            for e in range(E):
                at = sp.value_load(pad_at[0:1, e:e + 1], min_val=0, max_val=SPARE - SMALL)
                sp.dma_start(rows_x[bass.ds(at, SMALL), :].rearrange("(p k) r -> p (k r)", p=P),
                             pad_rows[:, :, :].rearrange("p k r -> p (k r)")).then_inc(padded, 16)
            sp.wait_ge(table_ready, 1)
            for par in range(RING):
                load_weights(par, par)
            sp.wait_ge(padded, 16 * (E + 1))
            sp.wait_ge(scattered, 16 * 2 * G * B)
            for par in range(RING):
                load_rows(par, par)

            def load(i, pos):
                j = CYCLE * i + pos
                wait_alone(sp, (tagged, j - RING + 1), (y_evac, FRONT + j - RING + 1))
                load_rows(j, pos)
                load_weights(j, pos % RING)

            for pos in range(RING, CYCLE):
                load(0, pos)
            with sp.Fori(1, CYCLES - 1) as i:
                for pos in range(CYCLE):
                    load(i, pos)
            for pos in range(CYCLE - 1):
                load(CYCLES - 1, pos)

            for par in range(RING):
                sp.wait_ge(y_sent[par], sent_in_all(par))

            def load_results(b, half):
                for k in range(2):
                    sp.dma_start(z_half[half][k], z_v[k, bass.ds(b, 1), :, half * TILE:(half + 1) * TILE]
                                 .rearrange("b p n -> (b p) n")).then_inc(z_loaded[half], 16)

            def store(b, half):
                sp.wait_ge(results_added, 2 * b + half + 1 - FRONT)
                sp.wait_ge(fin_ready, 2 * b + half + 1 - FRONT)
                sp.dma_start(out_v[bass.ds(b, 1), :, half * TILE:(half + 1) * TILE].rearrange("b p n -> (b p) n"),
                             res[:, bass.ds(b * G + K * half, K), :].rearrange("p g d -> p (g d)")).then_inc(stored, 16)

            for half in range(2):
                load_results(FRONT // 2, half)
            with sp.Fori(FRONT // 2, B - 1) as b:
                for half in range(2):
                    store(b, half)
                    load_results(b + 1, half)
            for half in range(2):
                store(B - 1, half)
            sp.wait_ge(stored, 16 * (SHARED_TILES - FRONT))

        @block.gpsimd
        def _(pool):
            def rstd_1(b0, b1):
                pool.wait_ge(ln1_moments, b1)
                rs = rstd[:, b0 * G:b1 * G]
                nc.gpsimd.tensor_scalar(rs, moments[:, b0 * G:b1 * G, 1], EPS_LN, None, ALU.add).then_inc(ln1_pool_step, b1 - b0)
                pool.wait_ge(ln1_pool_step, b1)
                nc.gpsimd.tensor_tensor(rs, rs, minus_half[:, 0:(b1 - b0) * G], ALU.pow).then_inc(ln1_rstd, b1 - b0)

            step = Chain(pool, const_step, 0)
            nc.gpsimd.iota(lw_mask[:, :].rearrange("p (g q) -> p g q", q=P), pattern=[[1, 2 * G - 1], [G, P]],
                           base=-(G - 1), channel_multiplier=-G, allow_small_or_imprecise_dtypes=True).then_inc(distance_ready, 1)
            step(nc.gpsimd.memset(minus_half[:, :], -0.5), wait=False)
            step(nc.gpsimd.memset(ident[:, :], 0.0), wait=False)
            step(nc.gpsimd.memset(offdiag[:, :], 1.0), wait=False)
            step(nc.gpsimd.memset(before[:, :], 1.0), wait=False)
            step(nc.gpsimd.memset(pad_rows[:, :, :], 0.0))
            step(nc.gpsimd.affine_select(out=ident[:, :], in_=ident[:, :], compare_op=ALU.not_equal, fill=1.0,
                                         base=0, pattern=[[-1, P]], channel_multiplier=1), wait=False)
            step(nc.gpsimd.affine_select(out=offdiag[:, :], in_=offdiag[:, :], compare_op=ALU.not_equal, fill=0.0,
                                         base=0, pattern=[[-1, P]], channel_multiplier=1), wait=False)
            step(nc.gpsimd.affine_select(out=before[:, :], in_=before[:, :], compare_op=ALU.is_gt, fill=0.0,
                                         base=0, pattern=[[1, P]], channel_multiplier=-1), wait=False)
            step(nc.gpsimd.memset(ones[:, :], 1.0), wait=False)
            step(nc.gpsimd.memset(h_ones[:, :, :, D:D + 1], 1.0), wait=False)
            pool.wait_ge(const_step, step.now())
            rstd_1(0, 1)
            step(nc.gpsimd.memset(carry[:, :], 0.0), wait=False)
            step(nc.gpsimd.memset(sums[:, :, :, :], 0.0), wait=False)
            step(nc.gpsimd.memset(earlier[:, 0, :], 0.0), wait=False)
            step(nc.gpsimd.iota(expert_no[:, :, :], pattern=[[0, G], [1, E]], base=0, channel_multiplier=0,
                                allow_small_or_imprecise_dtypes=True), wait=False)
            step(nc.gpsimd.iota(token_no[:, :], pattern=[[1, G]], base=0, channel_multiplier=G,
                                allow_small_or_imprecise_dtypes=True), wait=False)
            step(nc.gpsimd.iota(region_at[:, :], pattern=[[REGION, E]], base=0, channel_multiplier=0,
                                allow_small_or_imprecise_dtypes=True), wait=False)
            step(nc.gpsimd.iota(tile_no[:, :, :], pattern=[[1, LARGE_TILES], [0, E]], base=0, channel_multiplier=0,
                                allow_small_or_imprecise_dtypes=True), wait=False)
            step(nc.gpsimd.iota(pad_rows[:, :, D:D + 1].bitcast(I32), pattern=[[0, SMALL // P]], base=NOWHERE, channel_multiplier=0))
            nc.gpsimd.tensor_copy(carry[0:1, :], region_at[0:1, :]).then_inc(const_ready, 1)

            def modulation(b0, b1, start):
                pool.wait_ge(mod_evac, 2 * b1)
                step = Chain(pool, mod_step, start)
                for at in (0, 2):
                    shift_, scale = (mod[:, b0:b1, at + i, :] for i in range(2))
                    gate = att_gate[:, b0:b1, :] if at == 0 else mod[:, b0:b1, 4, :]
                    sz = half_sign[:, b0:b1, :]
                    step(nc.gpsimd.tensor_scalar(scale, scale, 1.0, None, ALU.add), wait=False)
                    step(nc.gpsimd.tensor_scalar(sz, gate, 0.0, -0.5, ALU.is_ge, ALU.add))
                    step(nc.gpsimd.tensor_tensor(gate, gate, sz, ALU.mult))
                    step(nc.gpsimd.tensor_scalar(gate, gate, 0.125, 4.0, ALU.max, ALU.mult))
                    step(nc.gpsimd.tensor_tensor(gate, gate, sz, ALU.mult))
                    if at == 0:
                        step(nc.gpsimd.tensor_tensor(scale, scale, gate, ALU.mult), wait=False)
                        step(nc.gpsimd.tensor_tensor(shift_, shift_, gate, ALU.mult))
                return start + step.n

            def gate_rows(b, par):
                pool.wait_ge(ln1_xhat, b + 1)
                wait(pool, value_step, G * (b - 1))
                h = h_ones[:, par, :, 0:D]
                scale = mod[:, bass.ds(b, 1), 1, :].to_broadcast([P, G, D])
                shift_ = mod[:, bass.ds(b, 1), 0, :].to_broadcast([P, G, D])
                nc.gpsimd.tensor_tensor(h, xhat[:, :, :], scale, ALU.mult).then_inc(gate_step, 1)
                pool.wait_ge(gate_step, b + 1)
                nc.gpsimd.tensor_tensor(h, h, shift_, ALU.add).then_inc(gated, 1)

            def rstd_2(b):
                wait_alone(pool, (ln2_moments, b + 1))
                nc.gpsimd.tensor_scalar(rstd2[:, :], moments2[:, :, 1], EPS_LN, None, ALU.add).then_inc(ln2_pool_step, 1)
                pool.wait_ge(ln2_pool_step, b + 1)
                nc.gpsimd.tensor_tensor(rstd2[:, :], rstd2[:, :], minus_half[:, 0:G], ALU.pow).then_inc(ln2_rstd, 1)

            def expert_rows(b):
                pool.wait_ge(ln2_xhat, b + 1)
                pool.wait_ge(h2t_ps_ready, 2 * b + 2)
                wait(pool, scattered, 16 * 2 * G * b)
                wait(pool, second_rows, b)
                scale = mod[:, bass.ds(b, 1), 3, :].to_broadcast([P, G, D])
                shift_ = mod[:, bass.ds(b, 1), 2, :].to_broadcast([P, G, D])
                nc.gpsimd.tensor_tensor(xhat2[:, :, :], xhat2[:, :, :], scale, ALU.mult).then_inc(ln2_mod_step, 1)
                pool.wait_ge(ln2_mod_step, b + 1)
                nc.gpsimd.tensor_tensor(row_1[:, :, 0:D], xhat2[:, :, :], shift_, ALU.add).then_inc(ln2_h, 1)

            def scatter(b, both_rows=(row_1, row_2), slot=slot, second=second_rows):
                wait_alone(pool, (slots_ready, b + 1))
                for k, rows in enumerate(both_rows):
                    if k == 1:
                        wait_alone(pool, (second, 1 if second is last_second else b + 1))
                    for g in range(G):
                        nc.gpsimd.indirect_dma_start(rows_x[:, :], bass.IndirectOffsetOnAxis(ap=slot[:, k, g:g + 1], axis=0),
                                                     rows[:, g, :], None).then_inc(scattered, 16)

            def batch(b, par):
                if exists(b + 1):
                    gate_rows(b + 1, 1 - par)
                if isinstance(b, int) and b == 0:
                    rstd_1(2, 3)
                    modulation(2, B, done)
                    rstd_1(3, AHEAD)
                if exists(b - 2):
                    expert_rows(b - 2)
                if exists(b - 1):
                    rstd_2(b - 1)
                if isinstance(b, int) and b == 1:
                    rstd_1(AHEAD, B)
                if exists(b - 2):
                    scatter(b - 2)

            rstd_1(1, 2)
            done = modulation(0, 1, 0)
            gate_rows(0, 0)
            done = modulation(1, 2, done)
            batches(pool, batch)
            rstd_2(B - 1)
            expert_rows(B - 2)
            scatter(B - 2)
            scatter(B - 1, (last_1, last_2), last_slot, last_second)

            def send(i, pos):
                par = pos % RING
                wait_alone(pool, (y_ready, CYCLE * i + pos + 1))
                for k in range(rows_of(pos) // P):
                    nc.gpsimd.indirect_dma_start(rows_z[:, :], bass.IndirectOffsetOnAxis(ap=tags[par][:, k, 0:1].bitcast(I32), axis=0),
                                                 tile_y[par][:, k, :], None, bounds_check=Z_ROWS - 1, oob_is_err=False).then_inc(y_sent[par], 16)

            with pool.Fori(0, CYCLES - 1) as i:
                for pos in range(CYCLE):
                    send(i, pos)
            for pos in range(CYCLE - 1):
                send(CYCLES - 1, pos)

            for par in range(RING):
                pool.wait_ge(y_sent[par], sent_in_all(par))
            pool.wait_ge(y_evac, FRONT)
            def load_front(b, par):
                for k in range(2):
                    nc.gpsimd.dma_start(z_front[par][k], z_v[k, bass.ds(b, 1), :, :].rearrange("b p n -> (b p) n")).then_inc(front_loaded[par], 16)

            def combine_front(b, i, par):
                pool.wait_ge(front_loaded[par], 32 * (i + 1))
                step = Chain(pool, front_step, 3 * b)
                gate = mod[:, bass.ds(b, 1), 4, :].to_broadcast([P, G, D])
                r = res[:, bass.ds(b * G, G), :]
                z0, z1 = (z.rearrange("p (g d) -> p g d", d=D) for z in z_front[par])
                step(nc.gpsimd.tensor_tensor(z0, z0, z1, ALU.add))
                step(nc.gpsimd.tensor_tensor(z0, z0, gate, ALU.mult))
                step(nc.gpsimd.tensor_tensor(r, r, z0, ALU.add), wait=False)
                wait_alone(pool, (front_step, step.now()))
                nc.gpsimd.dma_start(out_v[bass.ds(b, 1), :, :].rearrange("b p n -> (b p) n"),
                                    r.rearrange("p g d -> p (g d)")).then_inc(front_stored, 16)

            for b in range(2):
                load_front(b, b)
            with pool.Fori(0, FRONT // 4 - 1) as i:
                for par in range(2):
                    combine_front(2 * i + par, i, par)
                    load_front(2 * i + par + 2, par)
            for par in range(2):
                combine_front(FRONT // 2 - 2 + par, FRONT // 4 - 1, par)
            pool.wait_ge(front_stored, 16 * (FRONT // 2))

        @block.scalar
        def _(act):
            act.dma_start(c_sb[:, :], c_t).then_inc(cond_loaded, 16)
            act.dma_start(wmod_sb[:, :], wmod).then_inc(cond_loaded, 16)
            act.dma_start(watt_sb[:, :], w_att).then_inc(small_loaded, 16)
            act.dma_start(batt_sb[:, :], b_att).then_inc(small_loaded, 16)
            act.dma_start(wg_sb[:, :], wg).then_inc(small_loaded, 16)
            act.wait_ge(cond_loaded, 32)
            nc.scalar.activation(silu[:, :], c_sb[:, :], ACT.Exp, scale=-1.0).then_inc(silu_exp, 1)
            act.wait_ge(distance_ready, 1)
            nc.scalar.activation(lw[:, :], lw_mask[:, :], ACT.Abs).then_inc(distance_abs, 1)

            def modulation(n0, n1):
                for n in range(n0, n1):
                    act.wait_ge(mod_ps_ready, n + 1)
                    if n % 2 == 0:
                        nc.scalar.activation(att_gate[:, n // 2, :], value[:, n % 3, 2 * D:3 * D], ACT.Copy)
                        nc.scalar.activation(mod[:, n // 2, 0:2, :].rearrange("p m d -> p (m d)"),
                                             value[:, n % 3, 0:2 * D], ACT.Copy).then_inc(mod_evac, 1)
                    else:
                        nc.scalar.activation(mod[:, n // 2, 2:5, :].rearrange("p m d -> p (m d)"),
                                             value[:, n % 3, 0:3 * D], ACT.Copy).then_inc(mod_evac, 1)

            def normalise(b):
                act.wait_ge(ln1_ready, b + 1)
                wait(act, ht_ps_ready, 2 * b)
                wait_alone(act, (gated, b))
                for g in range(G):
                    at = b * G + g
                    ins = nc.scalar.activation(xhat[:, g, :], res[:, bass.ds(at, 1), :].rearrange("p o d -> p (o d)"), ACT.Identity,
                                               scale=rstd[:, bass.ds(at, 1)], bias=shift[:, bass.ds(at, 1)])
                ins.then_inc(ln1_xhat, 1)

            def transposed(b, par, half, bank=misc[:, :]):
                wait_alone(act, (ht_ps_ready, 2 * b + half + 1))
                at = slice(half * 512, half * 512 + 512)
                nc.scalar.activation(h_f[half], bank, ACT.Identity,
                                     scale=mod_col[:, 2, bass.ds(b, 1)], bias=mod_col[:, 0, bass.ds(b, 1)]).then_inc(ht_ready, 1)
                act.wait_ge(ht_ready, 2 * b + half + 1)
                nc.scalar.activation(h_hi[par][:, at], h_f[half], ACT.Copy).then_inc(h_hi_ready, 1)

            def queries(b, par, half, bank=misc[:, :]):
                act.wait_ge(qt_ps_ready, 2 * b + half + 1)
                nc.scalar.activation(q_hi[par][:, half * 512:half * 512 + 512], bank, ACT.Identity,
                                     bias=batt_sb[:, 0:1]).then_inc(q_hi_ready, 1)

            def weights(b, t):
                act.wait_ge(score_used, G * b + t + 1)
                nc.scalar.activation(prob[:, t % 4, :], prob[:, t % 4, :], ACT.Tanh).then_inc(tanh_done, 1)
                act.wait_ge(tanh_done, G * b + t + 1)
                nc.scalar.activation(prob[:, t % 4, :], prob[:, t % 4, :], ACT.Exp).then_inc(exp_done, 1)

            def second_copy(b):
                act.wait_ge(ln2_h, b + 1)
                nc.scalar.activation(row_2[:, :, 0:D], row_1[:, :, 0:D], ACT.Copy).then_inc(second_rows, 1)

            def stage_h2t(b, half, bank=misc[:, :]):
                wait(act, logits_ps_ready, b)
                wait(act, h2t_kept, b)
                wait_alone(act, (h2t_ps_ready, 2 * b + half + 1))
                nc.scalar.activation(h2_ts[:, half * 512:half * 512 + 512], bank, ACT.Identity,
                                     scale=mod_col[:, 3, bass.ds(b, 1)], bias=mod_col[:, 1, bass.ds(b, 1)]).then_inc(h2t_staged, 1)

            def keep_h2t(b):
                wait_alone(act, (h2t_staged, 2 * b + 2))
                nc.scalar.activation(h2_t[:, bass.ds(b * S, S)], h2_ts[:, :], ACT.Copy).then_inc(h2t_kept, 1)

            def gap_exponent(b):
                act.wait_ge(gap_ready, b + 1)
                nc.scalar.activation(gap_e[:, :], gap[:, :], ACT.Exp).then_inc(gap_exp, 1)

            def batch(b, par):
                if exists(b + 1) and not (isinstance(b, int) and b == 0):
                    transposed(b + 1, 1 - par, 0)
                weights(b, 0)
                if isinstance(b, int) and b == 0:
                    modulation(4, 7)
                    normalise(1)
                if exists(b - 2):
                    gap_exponent(b - 2)
                weights(b, 1)
                if isinstance(b, int) and b == 0:
                    modulation(7, 10)
                    transposed(1, 1, 0)
                    modulation(10, 2 * B)
                if exists(b + 1):
                    transposed(b + 1, 1 - par, 1)
                weights(b, 2)
                if exists(b + 1):
                    queries(b + 1, 1 - par, 0)
                weights(b, 3)
                if exists(b + 1):
                    queries(b + 1, 1 - par, 1)
                weights(b, 4)
                if exists(b - 2):
                    second_copy(b - 2)
                weights(b, 5)
                if exists(b - 1):
                    stage_h2t(b - 1, 0)
                weights(b, 6)
                if exists(b - 1):
                    stage_h2t(b - 1, 1)
                weights(b, 7)
                if exists(b - 1):
                    keep_h2t(b - 1)
                if exists(b + 2):
                    normalise(b + 2)

            normalise(0)
            act.wait_ge(col_ready, 1)
            for half in range(2):
                transposed(0, 0, half, score[:, half, :])
            act.wait_ge(small_loaded, 48)
            nc.scalar.activation(watt_hi[:, :], watt_sb[:, :], ACT.Copy).then_inc(watt_hi_ready, 1)
            modulation(0, 2)
            for half in range(2):
                queries(0, 0, half, score[:, 2 + half, :])
            modulation(2, 4)
            batches(act, batch)

            def split_x(n, par, src):
                wait(act, up_ready, C * (n - 1))
                rows = src.shape[-1]
                nc.scalar.activation(xt_hi[par][:, 0:rows], src, ACT.Copy).then_inc(x_hi_ready, 1)

            def split_w(par, w):
                nc.scalar.activation(w1_hi[par], w[:, 0:F], ACT.Copy).then_inc(w_hi_ready, 1)

            def relu(n, w, par, rows=TILE):
                for c in range(C):
                    act.wait_ge(up_ready, C * n + c + 1)
                    nc.scalar.activation(hidden[par][:, c, 0:rows], score[:, c, 0:rows], ACT.Relu,
                                         bias=w[:, B1_AT + c:B1_AT + c + 1]).then_inc(hidden_ready, 1)

            def shared_rows(n):
                return h2_t[:, n * TILE:(n + 1) * TILE]

            act.wait_ge(shared_loaded, 16)
            split_w(0, w_shared)
            split_x(0, 0, shared_rows(0))
            act.wait_ge(score_ready, G * B)
            split_x(1, 1, shared_rows(1))
            gap_exponent(B - 2)
            act.wait_ge(value_step, G * B)
            relu(0, w_shared, 0)
            split_x(2, 0, shared_rows(2))
            relu(1, w_shared, 1)
            split_x(3, 1, shared_rows(3))
            stage_h2t(B - 1, 0)
            stage_h2t(B - 1, 1, xt_ps)
            relu(2, w_shared, 0)
            split_x(4, 0, shared_rows(4))
            second_copy(B - 2)
            relu(3, w_shared, 1)
            split_x(5, 1, shared_rows(5))
            gap_exponent(B - 1)
            keep_h2t(B - 1)
            for n in range(4, FRONT):
                if 5 < n + 1 < FRONT:
                    split_x(n + 1, (n + 1) % 2, shared_rows(n + 1))
                relu(n, w_shared, n % 2)

            def expert_w(i, pos):
                act.wait_ge(w_loaded[pos % RING], loads(i, pos))
                act.wait_ge(up_ready, C * (FRONT + CYCLE * i + pos - 1))
                split_w((pos + 1) % 2, w_exp[pos % RING])

            def expert_x(i, pos):
                act.wait_ge(xt_ps_ready, CYCLE * i + pos + 1)
                split_x(FRONT + CYCLE * i + pos, pos % 2, xt_ps[:, 0:rows_of(pos)])

            def expert(i, pos):
                if rows_of(pos) == SMALL:
                    expert_w(*following(i, pos))
                relu(FRONT + CYCLE * i + pos, w_exp[pos % RING], pos % RING, rows_of(pos))
                if rows_of(pos) == TILE:
                    expert_w(*following(i, pos))
                expert_x(*following(i, pos))

            expert_w(0, 0)
            expert_x(0, 0)
            with act.Fori(0, CYCLES - 1) as i:
                for pos in range(CYCLE):
                    expert(i, pos)
            for pos in range(CYCLE - 2):
                expert(CYCLES - 1, pos)

            def split_rows(n, par, tile):
                wait_alone(act, (up_ready, C * (n - 1)))
                nc.scalar.activation(xt_hi[par], h2_t[:, bass.ds(tile * TILE, TILE)], ACT.Copy).then_inc(x_hi_ready, 1)

            def shared(b, half, last=False):
                n = ROW_TILES + 2 * b + half
                if not last:
                    split_rows(n + 1, (ROW_TILES + half + 1) % 2, 2 * b + half + 1)
                relu(n, w_shared, half)

            act.wait_ge(up_ready, C * (FRONT + ROW_TILES - 1))
            split_w((1 + ROW_TILES) % 2, w_shared)
            split_x(FRONT + ROW_TILES, (FRONT + ROW_TILES) % 2, shared_rows(FRONT))
            relu(FRONT + ROW_TILES - 1, w_exp[(CYCLE - 2) % RING], (CYCLE - 2) % RING)
            with act.Fori(FRONT // 2, B - 1) as b:
                for half in range(2):
                    shared(b, half)
            for half in range(2):
                shared(B - 1, half, last=(half == 1))

        @block.vector
        def _(dve):
            def moments_of(b, st, mom, chain, done, rows):
                step = Chain(dve, chain, b)
                wait_alone(dve, rows, (done, b))
                for g in range(G):
                    ins = nc.vector.bn_stats(st[:, g, :], res[:, bass.ds(b * G + g, 1), :].rearrange("p o d -> p (o d)"))
                step(ins, wait=False)
                wait_alone(dve, (step.sem, step.now()))
                for g in range(G):
                    ins = nc.vector.bn_aggr(mom[:, g, :], st[:, g, :])
                ins.then_inc(done, 1)

            def moments_1(b):
                moments_of(b, stats, moments[:, b * G:(b + 1) * G, :], ln1_step, ln1_moments,
                           (x_in[min(b, 2)], 16 * (1 if b < 2 else B - 2)))

            def shift_1(b0, b1):
                dve.wait_ge(ln1_rstd, b1)
                nc.vector.scalar_tensor_tensor(out=shift[:, b0 * G:b1 * G], in0=moments[:, b0 * G:b1 * G, 0], scalar=-1.0,
                                               in1=rstd[:, b0 * G:b1 * G], op0=ALU.mult, op1=ALU.mult).then_inc(ln1_ready, b1 - b0)

            def moments_2(b):
                moments_of(b, stats2, moments2, ln2_step, ln2_moments, (value_used, b + 1))

            moments_1(0)
            step = Chain(dve, silu_step, 0)
            dve.wait_ge(silu_exp, 1)
            step(nc.vector.tensor_scalar(silu[:, :], silu[:, :], 1.0, None, ALU.add))
            step(nc.vector.reciprocal(silu[:, :], silu[:, :]))
            step(nc.vector.tensor_tensor(silu[:, :], silu[:, :], c_sb[:, :], ALU.mult))
            nc.vector.tensor_copy(silu_b[:, :, :], silu[:, :].rearrange("p (b o) -> p b o", o=1).to_broadcast([P, B, P])).then_inc(silu_ready, 1)
            dve.wait_ge(col_ps_ready, 1)
            nc.vector.tensor_copy(mod_col[:, 0:2, :].rearrange("p m b -> p (m b)"), misc[:, 0:2 * B])
            nc.vector.tensor_scalar(mod_col[:, 2:4, :].rearrange("p m b -> p (m b)"), misc[:, 2 * B:4 * B], 1.0, None, ALU.add).then_inc(col_ready, 1)
            shift_1(0, 1)
            moments_1(1)
            lw_chain = Chain(dve, lw_step, 0)
            dve.wait_ge(distance_abs, 1)
            lw_chain(nc.vector.tensor_scalar(lw[:, :], lw[:, :], EPS_ATT, None, ALU.add))

            def location_weights(t):
                at = slice((G - 1 - t) * P, (G - t) * P)
                lw_chain(nc.vector.reciprocal(lw[:, at], lw[:, at]))
                lw_chain(nc.vector.scalar_tensor_tensor(out=lw[:, at], in0=lw_mask[:, at], scalar=0.0, in1=lw[:, at], op0=ALU.not_equal, op1=ALU.mult))

            def split_h(b, par, half):
                at = slice(half * 512, half * 512 + 512)
                dve.wait_ge(h_hi_ready, 2 * b + half + 1)
                nc.vector.tensor_tensor(h_lo[par][:, at], h_f[half], h_hi[par][:, at].bitcast(F32), ALU.subtract).then_inc(h_split, 1)

            def split_q(b, par, half, bank=misc[:, :]):
                at = slice(half * 512, half * 512 + 512)
                dve.wait_ge(q_hi_ready, 2 * b + half + 1)
                nc.vector.scalar_tensor_tensor(out=q_lo[par][:, at], in0=bank, scalar=batt_sb[:, 0:1], in1=q_hi[par][:, at].bitcast(F32),
                                               op0=ALU.add, op1=ALU.subtract).then_inc(qt_ready, 1)

            half_w = lw[:, (G - 1) * P:(G - 1) * P + S // 2], lw[:, (G - 1) * P + S // 2:(G - 1) * P + S]
            lw_chain(nc.vector.reciprocal(half_w[0], half_w[0]))
            dve.wait_ge(watt_hi_ready, 1)
            nc.vector.tensor_tensor(watt_lo[:, :], watt_sb[:, :], watt_hi[:, :].bitcast(F32), ALU.subtract).then_inc(watt_split, 1)
            for half in range(2):
                split_h(0, 0, half)
            lw_chain(nc.vector.reciprocal(half_w[1], half_w[1]))
            for half in range(2):
                split_q(0, 0, half, score[:, 2 + half, :])
            at = slice((G - 1) * P, (G - 1) * P + S)
            lw_chain(nc.vector.scalar_tensor_tensor(out=lw[:, at], in0=lw_mask[:, at], scalar=0.0, in1=lw[:, at], op0=ALU.not_equal, op1=ALU.mult))
            dve.wait_ge(const_ready, 1)
            nc.vector.memset(den[:, :], 0.0)
            shift_1(1, 2)

            def normalise_2(b, to=xhat2):
                dve.wait_ge(ln2_rstd, b + 1)
                if to is xhat2:
                    wait(dve, ln2_h, b)
                for g in range(G):
                    ins = nc.vector.tensor_scalar(to[:, g, :], res[:, bass.ds(b * G + g, 1), :].rearrange("p o d -> p (o d)"),
                                                  moments2[:, g, 0:1], rstd2[:, g:g + 1], ALU.subtract, ALU.mult)
                ins.then_inc(ln2_xhat, 1)

            def weigh(b, t):
                if isinstance(b, int) and b == 0 and t > 0:
                    location_weights(t)
                dve.wait_ge(score_ready, G * b + t + 1)
                wait(dve, value_step, G * b + t - 3)
                at = (G - 1 - t) * P
                nc.vector.tensor_tensor(prob[:, t % 4, :].rearrange("p (h n) -> p h n", h=2), score[:, 2 * (t % 2):2 * (t % 2) + 2, :],
                                        lw[:, at:at + S].rearrange("p (h n) -> p h n", h=2), ALU.mult).then_inc(score_used, 1)

            def clear_diagonal(b, t):
                dve.wait_ge(exp_done, G * b + t + 1)
                own = prob[:, t % 4, t * P:(t + 1) * P]
                nc.vector.tensor_tensor(own, own, offdiag[:, :], ALU.mult).then_inc(prob_ready, 1)

            def attend(b):
                dve.wait_ge(value_step, G * b + G)
                step = Chain(dve, att_step, b)
                for i in range(3):
                    n = min(3, G - 3 * i)
                    col = value[:, i, 0:n * (D + 1)].rearrange("p (s d) -> p s d", d=D + 1)[:, :, D]
                    ins = nc.vector.tensor_scalar(den[:, 3 * i:3 * i + n], col, EPS_ATT, None, ALU.add)
                step(ins)
                nc.vector.reciprocal(rden[:, :], den[:, :]).then_inc(rden_ready, 1)
                dve.wait_ge(rden_ready, b + 1)
                for s in range(G):
                    r = res[:, bass.ds(b * G + s, 1), :].rearrange("p o d -> p (o d)")
                    ins = nc.vector.scalar_tensor_tensor(out=r, in0=value_at(s), scalar=rden[:, s:s + 1], in1=r, op0=ALU.mult, op1=ALU.add)
                ins.then_inc(value_used, 1)

            def choose(b):
                dve.wait_ge(logits_ps_ready, b + 1)
                step = Chain(dve, route_step, ROUTE * b)
                nc.vector.tensor_copy(logits[:, :, :].rearrange("p g e -> p (g e)"), misc[:, 0:G * E]).then_inc(logits_ready, 1)
                wait_alone(dve, (logits_ready, b + 1))
                for g in range(G):
                    ins = nc.vector.max(top_v[:, g, :], logits[:, g, :])
                step(ins, wait=False)
                wait_alone(dve, (step.sem, step.now()))
                for g in range(G):
                    ins = nc.vector.max_index(top_i[:, g, :], top_v[:, g, :], logits[:, g, :])
                step(ins, wait=False)
                nc.vector.tensor_tensor(gap[:, :], top_v[:, :, 1], top_v[:, :, 0], ALU.subtract).then_inc(gap_ready, 1)
                dve.wait_ge(route_step, ROUTE * b + step.n)
                step(nc.vector.tensor_copy(top_f[:, :, :], top_i[:, :, :]))
                step(nc.vector.tensor_tensor(hot_1[:, :, :], expert_no[:, :, :], top_f[:, :, 0:1].to_broadcast([P, G, E]), ALU.is_equal), wait=False)
                step(nc.vector.tensor_tensor(hot_2[:, :, :], expert_no[:, :, :], top_f[:, :, 1:2].to_broadcast([P, G, E]), ALU.is_equal))
                step(nc.vector.tensor_tensor(chosen[:, :, :], hot_1[:, :, :], hot_2[:, :, :], ALU.add))
                wait(dve, rank_ps_ready, b)
                for g in range(G):
                    ins = nc.vector.tensor_tensor(earlier[:, g + 1, :], earlier[:, g, :], chosen[:, g, :], ALU.add)
                    if g < G - 1:
                        step(ins)
                ins.then_inc(chosen_ready, 1)
                assert step.n == CHOOSE, step.n

            def take_ranks(b):
                dve.wait_ge(rank_ps_ready, b + 1)
                rank = misc[:, 0:E].rearrange("p (o e) -> p o e", o=1).to_broadcast([P, G, E])
                nc.vector.tensor_tensor(place[:, :, :], earlier[:, 0:G, :], rank, ALU.add).then_inc(rank_used, 1)
                nc.vector.tensor_tensor(carry[:, :], carry[:, :], earlier[:, G, :], ALU.add).then_inc(carried, 1)

            def assign(b, both_rows=(row_1, row_2), slot=slot):
                first_rows, other_rows = both_rows
                """slots in the experts' regions, destinations and weights"""
                step = Chain(dve, route_step, ROUTE * b + CHOOSE)
                dve.wait_ge(rank_used, b + 1)
                dve.wait_ge(carried, b + 1)
                step(nc.vector.tensor_tensor(hot_1[:, :, :], hot_1[:, :, :], place[:, :, :], ALU.mult), wait=False)
                step(nc.vector.tensor_tensor(hot_2[:, :, :], hot_2[:, :, :], place[:, :, :], ALU.mult))
                step(nc.vector.tensor_reduce(slot_f[:, 0, :], hot_1[:, :, :], AX.X, ALU.add), wait=False)
                step(nc.vector.tensor_reduce(slot_f[:, 1, :], hot_2[:, :, :], AX.X, ALU.add))
                dve.wait_ge(gap_exp, b + 1)
                step(nc.vector.tensor_scalar(gap_1[:, :], gap_e[:, :], 1.0, None, ALU.add))
                step(nc.vector.reciprocal(w_first[:, :], gap_1[:, :]))
                step(nc.vector.tensor_tensor(w_second[:, :], w_first[:, :], gap_e[:, :], ALU.mult))
                dve.wait_ge(ln2_h, b + 1)
                step(nc.vector.tensor_copy(slot[:, :, :], slot_f[:, :, :]), wait=False)
                step(nc.vector.tensor_copy(first_rows[:, :, D + 1], w_first[:, :]), wait=False)
                step(nc.vector.tensor_copy(other_rows[:, :, D + 1], w_second[:, :]), wait=False)
                step(nc.vector.tensor_copy(first_rows[:, :, D].bitcast(I32), token_no[:, :]), wait=False)
                step(nc.vector.tensor_scalar(other_rows[:, :, D].bitcast(I32), token_no[:, :], float(T), None, ALU.add))
                nc.vector.tensor_scalar(token_no[:, :], token_no[:, :], float(S), None, ALU.add).then_inc(slots_ready, 1)
                dve.wait_ge(slots_ready, b + 1)
                assert CHOOSE + step.n == ROUTE, step.n

            def split_x(n, par, src):
                dve.wait_ge(x_hi_ready, n + 1)
                rows = src.shape[-1]
                nc.vector.tensor_tensor(xt_lo[par][:, 0:rows], src, xt_hi[par][:, 0:rows].bitcast(F32), ALU.subtract).then_inc(x_split, 1)

            def split_w(m, par, w):
                dve.wait_ge(w_hi_ready, m + 1)
                nc.vector.tensor_tensor(w1_lo[par], w[:, 0:F], w1_hi[par].bitcast(F32), ALU.subtract).then_inc(w_split, 1)

            def batch(b, par):
                weigh(b, 0)
                if isinstance(b, int) and b == 0:
                    moments_1(2)
                if isinstance(b, int) and b == 1:
                    moments_1(AHEAD)
                weigh(b, 1)
                if exists(b - 2):
                    take_ranks(b - 2)
                if exists(b - 1):
                    attend(b - 1)
                clear_diagonal(b, 0)
                weigh(b, 2)
                if exists(b + 1):
                    split_h(b + 1, 1 - par, 0)
                weigh(b, 3)
                clear_diagonal(b, 1)
                if exists(b + 1):
                    split_h(b + 1, 1 - par, 1)
                if exists(b - 1):
                    moments_2(b - 1)
                if exists(b + 1):
                    split_q(b + 1, 1 - par, 0)
                if isinstance(b, int) and b == 0:
                    moments_1(3)
                if isinstance(b, int) and b == 1:
                    moments_1(AHEAD + 1)
                clear_diagonal(b, 2)
                weigh(b, 4)
                if exists(b + 1):
                    split_q(b + 1, 1 - par, 1)
                clear_diagonal(b, 3)
                weigh(b, 5)
                clear_diagonal(b, 4)
                if exists(b - 1):
                    normalise_2(b - 1)
                if isinstance(b, int) and b == 0:
                    moments_1(4)
                if isinstance(b, int) and b == 1:
                    moments_1(AHEAD + 2)
                if exists(b - 2):
                    assign(b - 2)
                if isinstance(b, int) and b == 0:
                    shift_1(2, 3)
                if isinstance(b, int) and b == 1:
                    shift_1(3, AHEAD)
                weigh(b, 6)
                clear_diagonal(b, 5)
                weigh(b, 7)
                clear_diagonal(b, 6)
                if isinstance(b, int) and b == 1:
                    shift_1(AHEAD, B)
                if not exists(b + 1):
                    clear_diagonal(b, G - 1)
                    split_w(0, 0, w_shared)
                    split_x(0, 0, shared_rows(0))
                    split_x(1, 1, shared_rows(1))
                if exists(b - 1):
                    choose(b - 1)
                if exists(b + 1):
                    clear_diagonal(b, G - 1)

            def shared_rows(n):
                return h2_t[:, n * TILE:(n + 1) * TILE]

            def last_rows():
                dve.wait_ge(ln2_xhat, B)
                dve.wait_ge(h2t_ps_ready, 2 * B)
                dve.wait_ge(score_ready, G * B)
                step = Chain(dve, last_step, 0)
                scale = mod[:, B - 1:B, 3, :].to_broadcast([P, G, D])
                shift_ = mod[:, B - 1:B, 2, :].to_broadcast([P, G, D])
                dve.wait_ge(ln2_h, B - 1)
                step(nc.vector.tensor_tensor(xhat[:, :, :], xhat[:, :, :], scale, ALU.mult))
                nc.vector.tensor_tensor(last_1[:, :, 0:D], xhat[:, :, :], shift_, ALU.add).then_inc(ln2_h, 1)
                nc.vector.tensor_tensor(last_2[:, :, 0:D], xhat[:, :, :], shift_, ALU.add).then_inc(last_second, 1)

            batches(dve, batch)
            def shared(n):
                par, half = n % 2, n % 2
                dve.wait_ge(down_ready, n + 1)
                step = Chain(dve, y_step, 2 * n)
                bias = w_shared[:, B2_AT:PACK].rearrange("p (o d) -> p o d", o=1).to_broadcast([P, K, D])
                step(nc.vector.tensor_tensor(tile_y[par][:, :, :], yacc[par].rearrange("p (k d) -> p k d", k=K), bias, ALU.add))
                gate = mod[:, n // 2:n // 2 + 1, 4, :].to_broadcast([P, K, D])
                step(nc.vector.tensor_tensor(tile_y[par][:, :, :], tile_y[par][:, :, :], gate, ALU.mult))
                r = res[:, (n // 2) * G + K * half:(n // 2) * G + K * half + K, :]
                nc.vector.tensor_tensor(r, r, tile_y[par][:, :, :], ALU.add).then_inc(y_evac, 1)

            attend(B - 1)
            take_ranks(B - 2)
            moments_2(B - 1)
            split_x(2, 0, shared_rows(2))
            shared(0)
            dve.wait_ge(gated, B)
            dve.wait_ge(ht_ps_ready, 2 * B)
            normalise_2(B - 1, xhat)
            split_x(3, 1, shared_rows(3))
            assign(B - 2)
            last_rows()
            choose(B - 1)
            split_x(4, 0, shared_rows(4))
            shared(1)
            take_ranks(B - 1)
            shared(2)
            dve.wait_ge(total_ps_ready, 1)
            step = Chain(dve, table_step, 0)
            step(nc.vector.tensor_tensor(count[:, :], misc[:, 0:E], region_at[:, :], ALU.subtract))
            nc.vector.tensor_tensor(pad_at[:, :], count[:, :], region_at[:, :], ALU.add).then_inc(counted, 1)
            assign(B - 1, (last_1, last_2), last_slot)
            split_x(5, 1, shared_rows(5))
            shared(3)

            own, before_ = slice(E // 2, E // 2 + E), slice(E // 2 - 1, E // 2 + E - 1)

            def tiles_up_to(kind, rows, size, rounding):
                step(nc.vector.tensor_scalar(count_i[:, :], rows[:, :], float(rounding), None, ALU.add))
                step(nc.vector.tensor_scalar(tiles_i[:, :], count_i[:, :], size.bit_length() - 1, None, ALU.arith_shift_right))
                sum_of = [sums[:, kind, i, :] for i in range(4)]
                step(nc.vector.tensor_copy(sum_of[0][:, own], tiles_i[:, :]))
                for i in range(3):
                    by = slice(E // 2 - 2 ** i, E // 2 + E - 2 ** i)
                    step(nc.vector.tensor_tensor(sum_of[i + 1][:, own], sum_of[i][:, own], sum_of[i][:, by], ALU.add))
                return sum_of[3]

            def fill_table(kind, ends, size, limit):
                step(nc.vector.scalar_tensor_tensor(out=row_at[:, 0:E], in0=ends[:, before_], scalar=-float(size), in1=row_at[:, 0:E],
                                                    op0=ALU.mult, op1=ALU.add))
                step(nc.vector.tensor_tensor(row_step[:, :], row_at[:, 1:E + 1], row_at[:, 0:E], ALU.subtract))
                ends_b = ends[:, own].rearrange("p (o e) -> p o e", o=1).to_broadcast([P, LARGE_TILES, E])
                step_b = row_step[:, :].rearrange("p (o e) -> p o e", o=1).to_broadcast([P, LARGE_TILES, E])
                step(nc.vector.tensor_tensor(past[:, :, :], tile_no[:, :, :], ends_b, ALU.is_ge))
                step(nc.vector.tensor_reduce(tile_e[:, :], past[:, :, :], AX.X, ALU.add), wait=False)
                step(nc.vector.tensor_scalar(tile_r[:, :], tile_no[:, :, 0], float(size), row_at[:, 0:1], ALU.mult, ALU.add))
                step(nc.vector.tensor_scalar(table_e[:, :, kind], tile_e[:, :], float(E - 1), None, ALU.min), wait=False)
                step(nc.vector.tensor_tensor(past[:, :, :], past[:, :, :], step_b, ALU.mult))
                step(nc.vector.tensor_reduce(tile_e[:, :], past[:, :, :], AX.X, ALU.add))
                step(nc.vector.tensor_tensor(tile_r[:, :], tile_r[:, :], tile_e[:, :], ALU.add))
                return (nc.vector.tensor_scalar(table_r[:, :, kind], tile_r[:, :], float(limit), None, ALU.min))

            ends = tiles_up_to(0, count, TILE, 0)
            step(nc.vector.tensor_scalar(ends[:, own], ends[:, own], float(LARGE_TILES), None, ALU.min), wait=False)
            step(nc.vector.tensor_copy(row_at[:, 0:E], region_at[:, :]), wait=False)
            step(nc.vector.memset(row_at[:, E:E + 1], float(SPARE)))
            step(fill_table(0, ends, TILE, SPARE))
            step(nc.vector.tensor_tensor(rest[:, :], ends[:, own], ends[:, before_], ALU.subtract))
            step(nc.vector.scalar_tensor_tensor(out=row_at[:, 0:E], in0=rest[:, :], scalar=float(TILE), in1=region_at[:, :],
                                                op0=ALU.mult, op1=ALU.add), wait=False)
            step(nc.vector.scalar_tensor_tensor(out=rest[:, :], in0=rest[:, :], scalar=-float(TILE), in1=count[:, :],
                                                op0=ALU.mult, op1=ALU.add))
            split_x(6, 0, shared_rows(6))
            ends = tiles_up_to(1, rest, SMALL, SMALL - 1)
            shared(4)
            fill_table(1, ends, SMALL, SPARE).then_inc(table_ready, 1)

            split_x(7, 1, shared_rows(7))
            for n in range(5, FRONT - 1):
                shared(n)

            def add_bias(b):
                part = xhat2[:, 0:1, :]
                step = Chain(dve, bias_step, 2 * (b - FRONT // 2))
                bias = w_shared[:, B2_AT:PACK].rearrange("p (o d) -> p o d", o=1)
                step(nc.vector.tensor_tensor(part, mod[:, b:b + 1, 4, :], bias, ALU.mult))
                r = res[:, b * G:(b + 1) * G, :]
                step(nc.vector.tensor_tensor(r, r, part.to_broadcast([P, G, D]), ALU.add))

            def expert_split(i, pos):
                j = CYCLE * i + pos
                split_w(1 + j, (pos + 1) % 2, w_exp[pos % RING])
                split_x(FRONT + j, pos % 2, xt_ps[:, 0:rows_of(pos)])

            def expert(i, pos, last=False):
                j, par, groups = CYCLE * i + pos, pos % RING, rows_of(pos) // P
                if not last:
                    expert_split(*following(i, pos))
                else:
                    split_w(1 + ROW_TILES, (1 + ROW_TILES) % 2, w_shared)
                    split_x(FRONT + ROW_TILES, (FRONT + ROW_TILES) % 2, shared_rows(FRONT))
                wait(dve, y_sent[par], sent_before(i, pos))
                dve.wait_ge(down_ready, FRONT + j + 1)
                bias = w_exp[par][:, B2_AT:PACK].rearrange("p (o d) -> p o d", o=1).to_broadcast([P, groups, D])
                nc.vector.tensor_copy(tags[par][:, 0:groups, :], tile_x[par][:, 0:groups, D:ROW]).then_inc(tagged, 1)
                nc.vector.tensor_tensor(tile_y[par][:, 0:groups, :], yacc[par][:, 0:groups * D].rearrange("p (k d) -> p k d", k=groups),
                                        bias, ALU.add).then_inc(y_evac, 1)
                dve.wait_ge(tagged, j + 1)
                dve.wait_ge(y_evac, FRONT + j + 1)
                for k in range(groups):
                    ins = nc.vector.tensor_scalar(tile_y[par][:, k, :], tile_y[par][:, k, :], tags[par][:, k, 1:2], None, ALU.mult)
                ins.then_inc(y_ready, 1)

            expert_split(0, 0)
            shared(FRONT - 1)
            for pos in range(CYCLE):
                expert(0, pos)
                if 0 < pos <= B - FRONT // 2:
                    add_bias(FRONT // 2 - 1 + pos)
            with dve.Fori(1, CYCLES - 1) as i:
                for pos in range(CYCLE):
                    expert(i, pos)
            for pos in range(CYCLE - 1):
                expert(CYCLES - 1, pos, last=(pos == CYCLE - 2))

            def split_rows(b, half):
                dve.wait_ge(x_hi_ready, ROW_TILES + 2 * b + half + 2)
                par = (ROW_TILES + half + 1) % 2
                nc.vector.tensor_tensor(xt_lo[par], h2_t[:, bass.ds((2 * b + half + 1) * TILE, TILE)],
                                        xt_hi[par].bitcast(F32), ALU.subtract).then_inc(x_split, 1)

            def evacuate(b, half):
                n = ROW_TILES + 2 * b + half
                dve.wait_ge(down_ready, n + 1)
                y = tile_y[half][:, :, :]
                gate = mod[:, bass.ds(b, 1), 4, :].to_broadcast([P, K, D])
                nc.vector.tensor_tensor(y, yacc[half].rearrange("p (k d) -> p k d", k=K), gate, ALU.mult).then_inc(y_evac, 1)
                dve.wait_ge(y_evac, n + 1)
                wait(dve, results_added, 2 * b + half + 1 - FRONT if not isinstance(b, int) or 2 * b + half > FRONT else 0)
                r = res[:, bass.ds(b * G + K * half, K), :]
                nc.vector.tensor_tensor(r, r, y, ALU.add).then_inc(fin_ready, 1)

            def add_results(b, half):
                dve.wait_ge(z_loaded[half], 32 * (b - FRONT // 2 + 1))
                step = Chain(dve, fin_step, 2 * (2 * b + half - FRONT))
                z0, z1 = (z.rearrange("p (k d) -> p k d", k=K) for z in z_half[half])
                step(nc.vector.tensor_tensor(z0, z0, z1, ALU.add))
                gate = mod[:, bass.ds(b, 1), 4, :].to_broadcast([P, K, D])
                step(nc.vector.tensor_tensor(z0, z0, gate, ALU.mult))
                r = res[:, bass.ds(b * G + K * half, K), :]
                nc.vector.tensor_tensor(r, r, z0, ALU.add).then_inc(results_added, 1)

            split_rows(FRONT // 2, 0)
            for par in range(2):
                dve.wait_ge(y_sent[par], sent_in_all(par))
            evacuate(FRONT // 2, 0)
            split_rows(FRONT // 2, 1)
            dve.wait_ge(fin_ready, 1)
            add_results(FRONT // 2, 0)
            add_results(FRONT // 2, 1)
            evacuate(FRONT // 2, 1)
            with dve.Fori(FRONT // 2 + 1, B - 1) as b:
                for half in range(2):
                    split_rows(b, half)
                    add_results(b, half)
                    evacuate(b, half)
            split_rows(B - 1, 0)
            for half in range(2):
                add_results(B - 1, half)
                evacuate(B - 1, half)

        @block.tensor
        def _(pe):
            pe.wait_ge(cond_loaded, 32)
            pe.wait_ge(silu_ready, 1)
            for i, m in enumerate((0, 3, 1, 4)):
                ins = nc.tensor.matmul(misc[:, i * B:(i + 1) * B], wmod_sb[:, m * D:(m + 1) * D], silu[:, :], start=True, stop=True)
            ins.then_inc(col_ps_ready, 1)

            def modulation(n0, n1):
                for n in range(n0, n1):
                    if n >= 3:
                        pe.wait_ge(mod_evac, n - 2)
                    half = (n % 2) * (MOD // 2)
                    nc.tensor.matmul(value[:, n % 3, 0:MOD // 2], silu_b[:, n // 2, :], wmod_sb[:, half:half + MOD // 2],
                                     start=True, stop=True).then_inc(mod_ps_ready, 1)

            pe.wait_ge(const_ready, 1)

            def misc_rows(src, half, bank=misc):
                for k in range(4):
                    ins = nc.tensor.transpose(bank[:, k * P:(k + 1) * P], src[:, 4 * half + k, :], ident[:, :])
                return ins

            def transpose_h(b, half, bank=misc):
                pe.wait_ge(ln1_xhat, b + 1)
                if half and bank is misc:
                    pe.wait_ge(ht_ready, 2 * b + 1)
                if exists(b - 3):
                    pe.wait_ge(rank_used if half else logits_ready, b - 2)
                misc_rows(xhat, half, bank).then_inc(ht_ps_ready, 1)

            def product(out, left, right):
                (a_hi, a_lo), (b_hi, b_lo) = left, right
                nc.tensor.matmul(out, a_lo, b_hi, start=True, stop=False)
                nc.tensor.matmul(out, a_hi, b_lo, start=False, stop=False)
                return nc.tensor.matmul(out, a_hi, b_hi, start=False, stop=True)

            def queries(b, par, half, bank=misc):
                pe.wait_ge(h_split, 2 * b + 1 + half)
                if bank is misc:
                    pe.wait_ge(ht_ready if not half else qt_ready, 2 * b + 2 - half)
                at = slice(half * 512, half * 512 + 512)
                product(bank[:, :], (watt_hi[:, :], watt_lo[:, :]), (h_hi[par][:, at], h_lo[par][:, at])).then_inc(qt_ps_ready, 1)

            def scores(b, par, t):
                if t == 0:
                    pe.wait_ge(qt_ready, 2 * b + 2)
                wait(pe, score_used, G * b + t - 1)
                keys = slice(t * P, (t + 1) * P)
                for half in range(2):
                    at = slice(half * 512, half * 512 + 512)
                    ins = product(score[:, 2 * (t % 2) + half, :], (h_hi[par][:, keys], h_lo[par][:, keys]), (q_hi[par][:, at], q_lo[par][:, at]))
                ins.then_inc(score_ready, 1)

            def values(b, par, t):
                pe.wait_ge(prob_ready, G * b + t + 1)
                if t == 0:
                    pe.wait_ge(gated, b + 1)
                    wait(pe, value_used, b)
                for s in range(G):
                    c0 = (s % 3) * (D + 1)
                    ins = nc.tensor.matmul(value[:, s // 3, c0:c0 + D + 1], prob[:, t % 4, s * P:(s + 1) * P], h_ones[:, par, t, :],
                                           start=(t == 0 and s % 3 == 0), stop=(t == G - 1), skip_group_check=True)
                ins.then_inc(value_step, 1)

            def transpose_h2(b, half, bank=misc, rows=xhat2):
                pe.wait_ge(ln2_xhat, b + 1)
                if half and bank is misc:
                    pe.wait_ge(h2t_staged, 2 * b + 1)
                misc_rows(rows, half, bank).then_inc(h2t_ps_ready, 1)

            def gate_logits(b):
                pe.wait_ge(h2t_staged, 2 * b + 2)
                for g in range(G):
                    ins = nc.tensor.matmul(misc[:, g * E:(g + 1) * E], h2_ts[:, g * P:(g + 1) * P], wg_sb[:, :], start=True, stop=True)
                ins.then_inc(logits_ps_ready, 1)

            def ranks(b):
                pe.wait_ge(chosen_ready, b + 1)
                nc.tensor.matmul(misc[:, 0:E], before[:, :], earlier[:, G, :], start=True, stop=False)
                nc.tensor.matmul(misc[:, 0:E], ones[:, :], carry[:, :], start=False, stop=True).then_inc(rank_ps_ready, 1)

            def batch(b, par):
                scores(b, par, 0)
                if exists(b - 1):
                    values(b - 1, 1 - par, G - 2)
                if isinstance(b, int) and b == 0:
                    modulation(4, 7)
                elif exists(b + 1):
                    transpose_h(b + 1, 0)
                scores(b, par, 1)
                if exists(b - 1):
                    values(b - 1, 1 - par, G - 1)
                if exists(b - 2):
                    if exists(b + 1):
                        pe.wait_ge(ht_ready, 2 * b + 3)
                    ranks(b - 2)
                if isinstance(b, int) and b == 0:
                    modulation(7, 10)
                scores(b, par, 2)
                if isinstance(b, int) and b == 0:
                    transpose_h(1, 0)
                    modulation(10, 2 * B)
                if exists(b + 1):
                    transpose_h(b + 1, 1)
                if isinstance(b, int) and b == 0:
                    pe.wait_ge(mod_evac, 2 * B)
                scores(b, par, 3)
                values(b, par, 0)
                if exists(b + 1):
                    queries(b + 1, 1 - par, 0)
                scores(b, par, 4)
                values(b, par, 1)
                if exists(b + 1):
                    queries(b + 1, 1 - par, 1)
                scores(b, par, 5)
                values(b, par, 2)
                scores(b, par, 6)
                values(b, par, 3)
                if exists(b - 1):
                    if exists(b + 1):
                        pe.wait_ge(qt_ready, 2 * b + 4)
                    else:
                        pe.wait_ge(rank_used, b - 1)
                    transpose_h2(b - 1, 0)
                values(b, par, 4)
                if exists(b - 1):
                    transpose_h2(b - 1, 1)
                scores(b, par, 7)
                values(b, par, 5)
                if exists(b - 1):
                    gate_logits(b - 1)

            for half in range(2):
                transpose_h(0, half, score[:, half, :])
            modulation(0, 4)
            pe.wait_ge(watt_split, 1)
            for half in range(2):
                queries(0, 0, half, score[:, 2 + half, :])
            batches(pe, batch)
            values(B - 1, 1, G - 2)
            values(B - 1, 1, G - 1)

            def up(n, m, x_par, w_par, rows=TILE, first=False):
                pe.wait_ge(w_split, m + 1)
                pe.wait_ge(x_split, n + 1)
                for c in range(C):
                    if not first:
                        pe.wait_ge(hidden_ready, C * (n - 1) + c + 1)
                    at = slice(c * P, (c + 1) * P)
                    product(score[:, c, 0:rows], (w1_hi[w_par][:, at], w1_lo[w_par][:, at]),
                            (xt_hi[x_par][:, 0:rows], xt_lo[x_par][:, 0:rows])).then_inc(up_ready, 1)

            def down(n, w, par, rows=TILE, first=False):
                if not first:
                    pe.wait_ge(y_evac, n - 1)
                for c in range(C):
                    pe.wait_ge(hidden_ready, C * n + c + 1)
                    for k in range(rows // P):
                        ins = nc.tensor.matmul(yacc[par][:, k * D:(k + 1) * D], hidden[par][:, c, k * P:(k + 1) * P],
                                               w[:, W2_AT + c * D:W2_AT + (c + 1) * D],
                                               start=(c == 0 and k == 0), stop=(c == C - 1), skip_group_check=True)
                ins.then_inc(down_ready, 1)

            pe.wait_ge(h2t_kept, FRONT // 2)
            pe.wait_ge(shared_loaded, 16)
            pe.wait_ge(score_used, G * B)

            def shared_up(n):
                up(n, 0, n % 2, 0, first=(n == 0))

            def shared_down(n):
                down(n, w_shared, n % 2, first=(n < 2))

            shared_up(0)
            shared_up(1)
            ranks(B - 2)
            pe.wait_ge(value_used, B)
            shared_down(0)
            shared_down(1)
            shared_up(2)
            pe.wait_ge(rank_used, B - 1)
            transpose_h2(B - 1, 0, misc, xhat)
            transpose_h2(B - 1, 1, xt_ps, xhat)
            gate_logits(B - 1)
            shared_up(3)
            shared_down(2)
            ranks(B - 1)
            shared_up(4)
            pe.wait_ge(carried, B)
            nc.tensor.matmul(misc[:, 0:E], ones[:, :], carry[:, :], start=True, stop=True).then_inc(total_ps_ready, 1)
            shared_down(3)
            shared_down(4)
            for n in range(5, FRONT):
                shared_up(n)
                shared_down(n)
            pe.wait_ge(counted, 1)

            def transpose_rows(i, pos, first=False):
                par = pos % RING
                pe.wait_ge(x_loaded[par], loads(i, pos))
                if not first:
                    pe.wait_ge(x_split, FRONT + CYCLE * i + pos)
                for k in range(rows_of(pos) // P):
                    ins = nc.tensor.transpose(xt_ps[:, k * P:(k + 1) * P], tile_x[par][:, k, 0:D], ident[:, :])
                ins.then_inc(xt_ps_ready, 1)

            transpose_rows(0, 0, True)

            def expert(i, pos, last=False):
                j, par, rows = CYCLE * i + pos, pos % RING, rows_of(pos)
                up(FRONT + j, 1 + j, pos % 2, (pos + 1) % 2, rows)
                if not last:
                    transpose_rows(*following(i, pos))
                down(FRONT + j, w_exp[par], par, rows)

            with pe.Fori(0, CYCLES - 1) as i:
                for pos in range(CYCLE):
                    expert(i, pos)
            for pos in range(CYCLE - 1):
                expert(CYCLES - 1, pos, last=(pos == CYCLE - 2))

            pe.wait_ge(h2t_kept, B)
            with pe.Fori(FRONT // 2, B) as b:
                for half in range(2):
                    n = ROW_TILES + 2 * b + half
                    up(n, 1 + ROW_TILES, (ROW_TILES + half) % 2, (1 + ROW_TILES) % 2)
                    down(n, w_shared, half)


def kernel(**inputs):
    from concourse import bacc
    from concourse.bass_utils import run_bass_kernel_spmd

    a = {k.removeprefix("L0_"): np.asarray(v) for k, v in inputs.items()}

    def chunks(w):
        return w.reshape(C, P, D).transpose(1, 0, 2).reshape(P, C * D)

    def pack(w1, b1, w2, b2):
        return np.concatenate([w1, chunks(w2), b1.reshape(C, P).T, np.broadcast_to(b2, (P, D))], axis=1)

    packs = [pack(a["ffn_W1"][e], a["ffn_b1"][e], a["ffn_W2"][e], a["ffn_b2"][e]) for e in range(E)]
    packs.append(pack(a["ffn_Ws1"], a["ffn_bs1"], a["ffn_Ws2"], a["ffn_bs2"]))
    arrays = {
        "x": a["attn_x"].reshape(T, D), "c_t": a["c"].T, "wmod": a["wmod"], "w_att": a["attn_W"],
        "b_att": a["attn_b"].reshape(D, 1), "wg": a["ffn_Wg"], "packs": np.stack(packs),
    }
    arrays = {k: np.ascontiguousarray(v) for k, v in arrays.items()}
    nc = bacc.Bacc("TRN2", target_bir_lowering=False, num_devices=1)
    args = [nc.dram_tensor(k, v.shape, mybir.dt.from_np(v.dtype), kind="ExternalInput").ap() for k, v in arrays.items()]
    args.append(nc.dram_tensor("out", (T, D), F32, kind="ExternalOutput").ap())
    adaln_moe(nc, *args)
    r = run_bass_kernel_spmd(nc, [arrays], core_ids=[0])
    return r.results[0]["out"].reshape(B, S, D)
```
